# Optimizing a Trainium2 kernel written in Bass

```python
import numpy as np
import jax
import jax.numpy as jnp

def _softmax(x, axis=-1):
    return jax.nn.softmax(x, axis=axis)

def _gelu(x):
    return jax.nn.gelu(x, approximate=True)

def _silu(x):
    return jax.nn.silu(x)

def _sigmoid(x):
    return jax.nn.sigmoid(x)

def _layernorm(x, axis=-1, eps=1e-05):
    m = jnp.mean(x, axis=axis, keepdims=True)
    v = jnp.var(x, axis=axis, keepdims=True)
    return (x - m) / jnp.sqrt(v + eps)

def _scatter_add(tgt, idx, src, axis=0):
    return tgt.at[idx].add(src)

def _segment_sum(src, seg, n):
    return jax.ops.segment_sum(src, seg, n)
kernel_name = 'mk_prb_d2_jaxref_r8_c5fa6e'

def setup_inputs(seed: int=0):
    np.random.seed(seed)
    _w = jnp.asarray

    def _L0_attn_setup():
        import jax, jax.numpy as jnp
        import numpy as np
        import math
        EMBED_DIM = 128
        NHEAD = 16
        HEAD_DIM = 64
        BATCH = 2
        SEQ = 256
        key = jax.random.key(seed)
        k_in, k_wqkv, k_wo, k_g = jax.random.split(key, 4)
        std = math.sqrt(2.0 / EMBED_DIM)
        inputs = jax.random.normal(k_in, (BATCH, SEQ, EMBED_DIM), dtype=jnp.float32)
        Wqkv_w = jax.random.normal(k_wqkv, (3 * NHEAD * HEAD_DIM, EMBED_DIM), dtype=jnp.float32) * std
        Wqkv_b = jnp.zeros((3 * NHEAD * HEAD_DIM,), dtype=jnp.float32)
        Wo_w = jax.random.normal(k_wo, (EMBED_DIM, NHEAD * HEAD_DIM), dtype=jnp.float32) * std
        Wo_b = jnp.zeros((EMBED_DIM,), dtype=jnp.float32)
        ghost = jax.random.uniform(k_g, (NHEAD,), dtype=jnp.float32) * 0.1
        return {'inputs': inputs, 'Wqkv_w': Wqkv_w, 'Wqkv_b': Wqkv_b, 'Wo_w': Wo_w, 'Wo_b': Wo_b, 'ghost': ghost}
    _L0_attn_in = _L0_attn_setup()

    def _L0_ffn_setup():
        import jax, jax.numpy as jnp
        import numpy as np
        BLOCK = 16
        _GRID = jnp.array([0.0, 0.5, 1.0, 1.5, 2.0, 3.0, 4.0, 6.0], dtype=jnp.float32)
        _MID = jnp.array([0.25, 0.75, 1.25, 1.75, 2.5, 3.5, 5.0], dtype=jnp.float32)

        def fp4_quant_dequant(x):
            shape = x.shape
            xb = x.reshape(shape[:-1] + (shape[-1] // BLOCK, BLOCK))
            scale = jnp.max(jnp.abs(xb), axis=-1, keepdims=True) / 6.0
            scale = jnp.maximum(scale, jnp.float32(1e-12))
            xn = xb / scale
            idx = jnp.searchsorted(_MID, jnp.abs(xn))
            q = _GRID[idx] * jnp.sign(xn) * scale
            return q.reshape(shape)

        def fp4_linear(x, w):
            xq = fp4_quant_dequant(x)
            wq = fp4_quant_dequant(w)
            return jnp.einsum('bsk,nk->bsn', xq, wq)
        key = jax.random.key(seed)
        k1, k2, k3, k4 = jax.random.split(key, 4)
        H, I = (128, 352)
        x = jax.random.normal(k1, (4, 512, H), dtype=jnp.float32)
        w_gate = jax.random.normal(k2, (I, H), dtype=jnp.float32) * 0.02
        w_up = jax.random.normal(k3, (I, H), dtype=jnp.float32) * 0.02
        w_down = jax.random.normal(k4, (H, I), dtype=jnp.float32) * 0.02
        return {'x': x, 'w_gate': w_gate, 'w_up': w_up, 'w_down': w_down}
    _L0_ffn_in = _L0_ffn_setup()

    def _L1_attn_setup():
        import jax, jax.numpy as jnp
        import numpy as np
        NUM_BLOCKS = 8
        D = 128
        FF = 512
        B, S = (4, 512)
        EPS_ATTN = 1e-06
        EPS_LN = 1e-06

        def _ln(x, scale, bias):
            m = jnp.mean(x, axis=-1, keepdims=True)
            v = jnp.var(x, axis=-1, keepdims=True)
            return (x - m) * jax.lax.rsqrt(v + EPS_LN) * scale + bias

        def _forward(x, Wq, bq, Wk, bk, Wv, bv, Wo, bo, ln1_s, ln1_b, W1, b1, W2, b2, ln2_s, ln2_b):
            gelu = lambda t: jax.nn.gelu(t, approximate=True)
            fmap = lambda t: jax.nn.elu(t) + 1.0
            for i in range(NUM_BLOCKS):
                residual = x
                Q = fmap(x @ Wq[i] + bq[i])
                K = fmap(x @ Wk[i] + bk[i])
                value = x @ Wv[i] + bv[i]
                KV = jnp.einsum('nsh,nsh->nh', K, value)
                Ksum = jnp.sum(K, axis=1)
                Z = 1.0 / (Q * Ksum[:, None, :] + EPS_ATTN)
                V = Q * KV[:, None, :] * Z
                attn_out = gelu(V @ Wo[i] + bo[i])
                x = _ln(attn_out + residual, ln1_s[i], ln1_b[i])
                residual = x
                h = gelu(x @ W1[i] + b1[i])
                ff_out = gelu(h @ W2[i] + b2[i])
                x = _ln(ff_out + residual, ln2_s[i], ln2_b[i])
            return x
        key = jax.random.key(seed)
        ks = jax.random.split(key, 16)
        g = lambda k, shape, fan: jax.random.normal(k, shape, jnp.float32) * (1.0 / np.sqrt(fan))
        inp = {'x': jax.random.normal(ks[0], (B, S, D), jnp.float32), 'Wq': g(ks[1], (NUM_BLOCKS, D, D), D), 'bq': jnp.zeros((NUM_BLOCKS, D), jnp.float32), 'Wk': g(ks[2], (NUM_BLOCKS, D, D), D), 'bk': jnp.zeros((NUM_BLOCKS, D), jnp.float32), 'Wv': g(ks[3], (NUM_BLOCKS, D, D), D), 'bv': jnp.zeros((NUM_BLOCKS, D), jnp.float32), 'Wo': g(ks[4], (NUM_BLOCKS, D, D), D), 'bo': jnp.zeros((NUM_BLOCKS, D), jnp.float32), 'ln1_s': jnp.ones((NUM_BLOCKS, D), jnp.float32), 'ln1_b': jnp.zeros((NUM_BLOCKS, D), jnp.float32), 'W1': g(ks[5], (NUM_BLOCKS, D, FF), D), 'b1': jnp.zeros((NUM_BLOCKS, FF), jnp.float32), 'W2': g(ks[6], (NUM_BLOCKS, FF, D), FF), 'b2': jnp.zeros((NUM_BLOCKS, D), jnp.float32), 'ln2_s': jnp.ones((NUM_BLOCKS, D), jnp.float32), 'ln2_b': jnp.zeros((NUM_BLOCKS, D), jnp.float32)}
        return inp
    _L1_attn_in = _L1_attn_setup()

    def _L1_ffn_setup():
        import jax, jax.numpy as jnp
        import numpy as np
        D_MODEL, D_FF, N_EXPERTS, TOP_K = (128, 512, 8, 2)
        key = jax.random.key(seed)
        ks = jax.random.split(key, 7)
        s = 0.02
        return {'x': jax.random.normal(ks[0], (2, 256, D_MODEL), dtype=jnp.float32), 'router_w': jax.random.normal(ks[1], (D_MODEL, N_EXPERTS), dtype=jnp.float32) * s, 'router_b': jnp.zeros((N_EXPERTS,), dtype=jnp.float32), 'w1': jax.random.normal(ks[2], (N_EXPERTS, D_MODEL, D_FF), dtype=jnp.float32) * s, 'b1': jnp.zeros((N_EXPERTS, D_FF), dtype=jnp.float32), 'w2': jax.random.normal(ks[3], (N_EXPERTS, D_FF, D_MODEL), dtype=jnp.float32) * s, 'b2': jnp.zeros((N_EXPERTS, D_MODEL), dtype=jnp.float32)}
    _L1_ffn_in = _L1_ffn_setup()
    _d = {'L0_attn_inputs': _L0_attn_in['inputs'], 'L0_attn_Wqkv_w': _L0_attn_in['Wqkv_w'], 'L0_attn_Wqkv_b': _L0_attn_in['Wqkv_b'], 'L0_attn_Wo_w': _L0_attn_in['Wo_w'], 'L0_attn_Wo_b': _L0_attn_in['Wo_b'], 'L0_attn_ghost': _L0_attn_in['ghost'], 'L0_ffn_w_gate': _L0_ffn_in['w_gate'], 'L0_ffn_w_up': _L0_ffn_in['w_up'], 'L0_ffn_w_down': _L0_ffn_in['w_down'], 'L1_attn_Wq': _L1_attn_in['Wq'], 'L1_attn_bq': _L1_attn_in['bq'], 'L1_attn_Wk': _L1_attn_in['Wk'], 'L1_attn_bk': _L1_attn_in['bk'], 'L1_attn_Wv': _L1_attn_in['Wv'], 'L1_attn_bv': _L1_attn_in['bv'], 'L1_attn_Wo': _L1_attn_in['Wo'], 'L1_attn_bo': _L1_attn_in['bo'], 'L1_attn_ln1_s': _L1_attn_in['ln1_s'], 'L1_attn_ln1_b': _L1_attn_in['ln1_b'], 'L1_attn_W1': _L1_attn_in['W1'], 'L1_attn_b1': _L1_attn_in['b1'], 'L1_attn_W2': _L1_attn_in['W2'], 'L1_attn_b2': _L1_attn_in['b2'], 'L1_attn_ln2_s': _L1_attn_in['ln2_s'], 'L1_attn_ln2_b': _L1_attn_in['ln2_b'], 'L1_ffn_router_w': _L1_ffn_in['router_w'], 'L1_ffn_router_b': _L1_ffn_in['router_b'], 'L1_ffn_w1': _L1_ffn_in['w1'], 'L1_ffn_b1': _L1_ffn_in['b1'], 'L1_ffn_w2': _L1_ffn_in['w2'], 'L1_ffn_b2': _L1_ffn_in['b2']}
    _x0 = _d['L0_attn_inputs']
    _d['L0_attn_inputs'] = jax.random.normal(jax.random.fold_in(jax.random.key(seed), 1), (4, 1024, 128), dtype=_x0.dtype)
    del _x0
    return _d

def reference(L0_attn_inputs, L0_attn_Wqkv_w, L0_attn_Wqkv_b, L0_attn_Wo_w, L0_attn_Wo_b, L0_attn_ghost, L0_ffn_w_gate, L0_ffn_w_up, L0_ffn_w_down, L1_attn_Wq, L1_attn_bq, L1_attn_Wk, L1_attn_bk, L1_attn_Wv, L1_attn_bv, L1_attn_Wo, L1_attn_bo, L1_attn_ln1_s, L1_attn_ln1_b, L1_attn_W1, L1_attn_b1, L1_attn_W2, L1_attn_b2, L1_attn_ln2_s, L1_attn_ln2_b, L1_ffn_router_w, L1_ffn_router_b, L1_ffn_w1, L1_ffn_b1, L1_ffn_w2, L1_ffn_b2):

    def _L0_attn_ref(inputs, Wqkv_w, Wqkv_b, Wo_w, Wo_b, ghost):
        import jax, jax.numpy as jnp
        import numpy as np
        import math
        EMBED_DIM = 128
        NHEAD = 16
        HEAD_DIM = 64
        BATCH = 2
        SEQ = 256
        b, s, e = inputs.shape
        QKV = inputs @ Wqkv_w.T + Wqkv_b
        QKVh = QKV.reshape(b, s, 3, NHEAD, HEAD_DIM).transpose(0, 3, 2, 1, 4)
        Q, K, V = (QKVh[:, :, 0], QKVh[:, :, 1], QKVh[:, :, 2])
        scores = jnp.einsum('bhqd,bhkd->bhqk', Q, K) / math.sqrt(HEAD_DIM)
        row = jnp.arange(s)
        mask = jnp.where(row[None, :] > row[:, None], -jnp.inf, 0.0).astype(scores.dtype)
        scores = scores + mask[None, None]
        m = jnp.max(scores, axis=-1, keepdims=True)
        z = jnp.exp(scores - m)
        S = z / (jnp.sum(z, axis=-1, keepdims=True) + ghost.reshape(1, -1, 1, 1))
        A = jnp.einsum('bhqk,bhkd->bhqd', S, V)
        A = A.transpose(0, 2, 1, 3).reshape(b, s, NHEAD * HEAD_DIM)
        return A @ Wo_w.T + Wo_b

    def _L0_ffn_ref(x, w_gate, w_up, w_down):
        import jax, jax.numpy as jnp
        import numpy as np
        BLOCK = 16
        _GRID = jnp.array([0.0, 0.5, 1.0, 1.5, 2.0, 3.0, 4.0, 6.0], dtype=jnp.float32)
        _MID = jnp.array([0.25, 0.75, 1.25, 1.75, 2.5, 3.5, 5.0], dtype=jnp.float32)

        def fp4_quant_dequant(x):
            shape = x.shape
            xb = x.reshape(shape[:-1] + (shape[-1] // BLOCK, BLOCK))
            scale = jnp.max(jnp.abs(xb), axis=-1, keepdims=True) / 6.0
            scale = jnp.maximum(scale, jnp.float32(1e-12))
            xn = xb / scale
            idx = jnp.searchsorted(_MID, jnp.abs(xn))
            q = _GRID[idx] * jnp.sign(xn) * scale
            return q.reshape(shape)

        def fp4_linear(x, w):
            xq = fp4_quant_dequant(x)
            wq = fp4_quant_dequant(w)
            return jnp.einsum('bsk,nk->bsn', xq, wq)
        gate = fp4_linear(x, w_gate)
        y = fp4_linear(x, w_up)
        h = jax.nn.silu(gate) * y
        return fp4_linear(h, w_down)

    def _L1_attn_ref(x, Wq, bq, Wk, bk, Wv, bv, Wo, bo, ln1_s, ln1_b, W1, b1, W2, b2, ln2_s, ln2_b):
        import jax, jax.numpy as jnp
        import numpy as np
        NUM_BLOCKS = 8
        D = 128
        FF = 512
        B, S = (4, 512)
        EPS_ATTN = 1e-06
        EPS_LN = 1e-06

        def _ln(x, scale, bias):
            m = jnp.mean(x, axis=-1, keepdims=True)
            v = jnp.var(x, axis=-1, keepdims=True)
            return (x - m) * jax.lax.rsqrt(v + EPS_LN) * scale + bias

        def _forward(x, Wq, bq, Wk, bk, Wv, bv, Wo, bo, ln1_s, ln1_b, W1, b1, W2, b2, ln2_s, ln2_b):
            gelu = lambda t: jax.nn.gelu(t, approximate=True)
            fmap = lambda t: jax.nn.elu(t) + 1.0
            for i in range(NUM_BLOCKS):
                residual = x
                Q = fmap(x @ Wq[i] + bq[i])
                K = fmap(x @ Wk[i] + bk[i])
                value = x @ Wv[i] + bv[i]
                KV = jnp.einsum('nsh,nsh->nh', K, value)
                Ksum = jnp.sum(K, axis=1)
                Z = 1.0 / (Q * Ksum[:, None, :] + EPS_ATTN)
                V = Q * KV[:, None, :] * Z
                attn_out = gelu(V @ Wo[i] + bo[i])
                x = _ln(attn_out + residual, ln1_s[i], ln1_b[i])
                residual = x
                h = gelu(x @ W1[i] + b1[i])
                ff_out = gelu(h @ W2[i] + b2[i])
                x = _ln(ff_out + residual, ln2_s[i], ln2_b[i])
            return x
        return _forward(x, Wq, bq, Wk, bk, Wv, bv, Wo, bo, ln1_s, ln1_b, W1, b1, W2, b2, ln2_s, ln2_b)

    def _L1_ffn_ref(x, router_w, router_b, w1, b1, w2, b2):
        import jax, jax.numpy as jnp
        import numpy as np
        D_MODEL, D_FF, N_EXPERTS, TOP_K = (128, 512, 8, 2)
        bsz, seq_len, d_model = x.shape
        flat_x = x.reshape(-1, d_model)
        logits = flat_x @ router_w + router_b
        topk_scores, topk_idx = jax.lax.top_k(logits, TOP_K)
        gates = jax.nn.softmax(topk_scores, axis=-1).astype(flat_x.dtype)
        mixed = jnp.zeros_like(flat_x)
        num_experts = w1.shape[0]
        for e in range(num_experts):
            h = jax.nn.gelu(flat_x @ w1[e] + b1[e], approximate=False)
            y = h @ w2[e] + b2[e]
            w_e = jnp.sum(jnp.where(topk_idx == e, gates, 0.0), axis=-1, keepdims=True)
            mixed = mixed + w_e * y
        return mixed.reshape(bsz, seq_len, d_model)
    x = L0_attn_inputs
    xn = _layernorm(x, axis=-1)
    x = x + _L0_attn_ref(xn, L0_attn_Wqkv_w, L0_attn_Wqkv_b, L0_attn_Wo_w, L0_attn_Wo_b, L0_attn_ghost) + _L0_ffn_ref(xn, L0_ffn_w_gate, L0_ffn_w_up, L0_ffn_w_down)
    xn = _layernorm(x, axis=-1)
    x = x + _L1_attn_ref(xn, L1_attn_Wq, L1_attn_bq, L1_attn_Wk, L1_attn_bk, L1_attn_Wv, L1_attn_bv, L1_attn_Wo, L1_attn_bo, L1_attn_ln1_s, L1_attn_ln1_b, L1_attn_W1, L1_attn_b1, L1_attn_W2, L1_attn_b2, L1_attn_ln2_s, L1_attn_ln2_b) + _L1_ffn_ref(xn, L1_ffn_router_w, L1_ffn_router_b, L1_ffn_w1, L1_ffn_b1, L1_ffn_w2, L1_ffn_b2)
    return x

_drawn_inputs = setup_inputs


def setup_inputs(seed=0):
    import zlib

    import numpy as np

    out = dict(_drawn_inputs(seed))
    spreads = {'L0_attn_Wqkv_b': (0.0, 0.1),
     'L0_attn_Wo_b': (0.0, 0.484),
     'L1_attn_bq': (0.0, 2.0),
     'L1_attn_bk': (0.0, 2.0),
     'L1_attn_bv': (0.0, 0.1),
     'L1_attn_bo': (0.0, 0.1),
     'L1_attn_ln1_s': (1.0, 0.2),
     'L1_attn_ln1_b': (0.0, 0.1),
     'L1_attn_b1': (0.0, 0.354),
     'L1_attn_b2': (0.0, 0.1),
     'L1_attn_ln2_s': (1.0, 0.2),
     'L1_attn_ln2_b': (0.0, 0.1),
     'L1_ffn_router_b': (0.0, 0.383),
     'L1_ffn_b1': (0.0, 0.8),
     'L1_ffn_b2': (0.0, 0.806)}
    factors = {'L0_attn_ghost': 16.027,
     'L0_ffn_w_gate': 8.0,
     'L0_ffn_w_up': 8.0,
     'L0_ffn_w_down': 8.0,
     'L1_attn_Wq': 26.82,
     'L1_ffn_w1': 4.0,
     'L1_ffn_w2': 3.593}
    for name, (base, spread) in spreads.items():
        noise = np.random.default_rng([zlib.crc32(name.encode()), seed]).standard_normal(out[name].shape)
        drawn = base * np.exp(spread * noise) if base else spread * noise
        out[name] = jnp.asarray(drawn.astype(out[name].dtype))
    for name, factor in factors.items():
        out[name] = (out[name] * factor).astype(out[name].dtype)
    return out
```

```python
from contextlib import ExitStack

import concourse.bass as bass
from concourse import mybir

ALU = mybir.AluOpType
ACT = mybir.ActivationFunctionType
AX = mybir.AxisListType
F32 = mybir.dt.float32
F32R = mybir.dt.float32r
BF16 = mybir.dt.bfloat16
U32 = mybir.dt.uint32

P = 128
BATCH, SEQ, D = 4, 1024, 128
TILES = BATCH * SEQ // P
TB = SEQ // P
CH = 512
CHUNKS = BATCH * SEQ // CH
TC = CH // P
HEADS, DH = 16, 64
PAIRS = HEADS // 2
INNER = 352
IC = [(0, 128), (128, 128), (256, 96)]
QB = 16
LAYERS, FF, FC = 8, 512, 4
EXPERTS = 8
EPS_OUTER, EPS_LN, EPS_ATTN = 1e-5, 1e-6, 1e-6
MASKED = -1e30


class Count:

    def __init__(self, ctx, nc, name, per_turn=0, credit=0):
        self.sem = ctx.enter_context(nc.semaphore(name))
        self.per_turn, self.credit = per_turn, credit

    def at(self, turn, n):
        return turn * self.per_turn + (n + self.credit)


def sbuf(ctx, nc, name, shape, dt=F32):
    return ctx.enter_context(nc.sbuf_tensor(name, shape, dt))


def psum(ctx, nc, name, shape, dt=F32):
    return ctx.enter_context(nc.psum_tensor(name, shape, dt))


class Chain:

    def __init__(self, eng, count, turn=0):
        self.eng, self.count, self.turn, self.n = eng, count, turn, 0

    def link(self, ins):
        self.n += 1
        ins.then_inc(self.count.sem, 1)
        self.eng.wait_ge(self.count.sem, self.count.at(self.turn, self.n))


HALVES, ONES, TWOS = 1.5 * 2 ** 22, 1.5 * 2 ** 23, 1.5 * 2 ** 24
BELOW = 1.0 - 2.0 ** -24


def fp4_round_trip(dve, chain, src, dst, bmax, scale, rinv, t0, t1, t2, t3, nb):
    def blocks(t):
        return t.rearrange("p (n q) -> p n q", q=QB)

    def spread(t):
        return t.unsqueeze(2).broadcast_to([t.shape[0], nb, QB])

    link = chain.link
    link(dve.tensor_reduce(bmax, blocks(src), AX.X, ALU.max, apply_absolute_value=True))
    link(dve.tensor_scalar(scale, bmax, 1.0 / 6.0, 1e-12, ALU.mult, ALU.max))
    link(dve.reciprocal(rinv, scale))
    link(dve.tensor_scalar(rinv, rinv, BELOW, None, ALU.mult))
    link(dve.tensor_tensor(blocks(t0), blocks(src), spread(rinv), ALU.mult))
    link(dve.tensor_scalar(t0.bitcast(U32), t0.bitcast(U32), 0x7FFFFFFF, None, ALU.bitwise_and))
    link(dve.tensor_scalar(t1, t0, 2.0, HALVES, ALU.min, ALU.add))
    link(dve.tensor_scalar(t2, t0, 2.0, ONES, ALU.max, ALU.add))
    link(dve.tensor_scalar(t3, t0, 4.0, TWOS, ALU.max, ALU.add))
    link(dve.tensor_scalar(t2, t2, ONES + 4.0, ONES, ALU.min, ALU.subtract))
    link(dve.scalar_tensor_tensor(out=t1, in0=t1, scalar=HALVES, in1=t2, op0=ALU.subtract, op1=ALU.add))
    link(dve.scalar_tensor_tensor(out=t0, in0=t3, scalar=TWOS + 6.0, in1=t1, op0=ALU.subtract, op1=ALU.add))
    link(dve.scalar_tensor_tensor(out=t2.bitcast(U32), in0=src.bitcast(U32), scalar=0x80000000,
                                  in1=t0.bitcast(U32), op0=ALU.bitwise_and, op1=ALU.bitwise_or))
    link(dve.tensor_tensor(blocks(dst), blocks(t2), spread(scale), ALU.mult))


FP4_LINKS = 14


def inverse_root(dve, chain, out, var, root, eps, half, t0):
    link = chain.link
    link(dve.reciprocal(out, root))
    link(dve.tensor_scalar(half, var, eps, -0.5, ALU.add, ALU.mult))
    link(dve.tensor_tensor(t0, out, out, ALU.mult))
    link(dve.tensor_tensor(t0, t0, half, ALU.mult))
    link(dve.scalar_tensor_tensor(out=out, in0=t0, scalar=1.5, in1=out, op0=ALU.add, op1=ALU.mult))


ROOT_LINKS = 5


def build_constants(nc, k):
    with ExitStack() as ctx:
        made = Count(ctx, nc, "constants_made")
        block = ctx.enter_context(nc.Block())

        @block.gpsimd
        def _(pool):
            pool.memset(k.ident[:], 0.0).then_inc(made.sem, 1)
            pool.memset(k.maskb[:], 0.0).then_inc(made.sem, 1)
            pool.memset(k.eps_outer[:], EPS_OUTER).then_inc(made.sem, 1)
            pool.memset(k.eps_ln[:], EPS_LN).then_inc(made.sem, 1)
            pool.memset(k.identb[:], 0.0).then_inc(made.sem, 1)
            pool.wait_ge(made.sem, 5)
            for t in (k.ident, k.identb):
                pool.affine_select(out=t[:], in_=t[:], compare_op=ALU.not_equal, fill=1.0, base=0,
                                   pattern=[[-1, P]], channel_multiplier=1)
            pool.affine_select(out=k.maskb[:], in_=k.maskb[:], compare_op=ALU.is_ge, fill=MASKED, base=0,
                               pattern=[[-1, P]], channel_multiplier=1)


def outer_statistics(nc, k, name):
    with ExitStack() as ctx:
        stats = sbuf(ctx, nc, f"{name}_stats", [P, TILES, 6])
        root = sbuf(ctx, nc, f"{name}_root", [P, TILES])
        half = sbuf(ctx, nc, f"{name}_half", [P, TILES])
        t0 = sbuf(ctx, nc, f"{name}_t0", [P, TILES])
        stat = Count(ctx, nc, f"{name}_stat")
        aggregated = Count(ctx, nc, f"{name}_aggregated")
        rooted = Count(ctx, nc, f"{name}_rooted")
        steps = Count(ctx, nc, f"{name}_steps")
        block = ctx.enter_context(nc.Block())

        @block.vector
        def _(dve):
            with dve.Fori(0, TILES // TC) as c:
                for t in range(TC):
                    dve.bn_stats(stats[:, bass.ds(c * TC + t, 1), :], k.resid[:, bass.ds(c * TC + t, 1), :])\
                       .then_inc(stat.sem, 1)
            dve.wait_ge(stat.sem, TILES)
            for t in range(TILES):
                ins = dve.bn_aggr(k.mv[:, t, :], stats[:, t, :])
            ins.then_inc(aggregated.sem, 1)
            dve.wait_ge(rooted.sem, 1)
            inverse_root(dve, Chain(dve, steps), k.rstd[:], k.mv[:, :, 1], root[:], EPS_OUTER, half[:], t0[:])

        @block.scalar
        def _(act):
            act.wait_ge(aggregated.sem, 1)
            act.activation(root[:], k.mv[:, :, 1], ACT.Sqrt, bias=k.eps_outer[:]).then_inc(rooted.sem, 1)


def normalise_chunk(dve, k, c, xn, done):
    for t in range(TC):
        i = c * TC + t
        dve.tensor_scalar(xn[:, t, :], k.resid[:, bass.ds(i, 1), :].rearrange("p a d -> p (a d)"),
                          k.mv[:, bass.ds(i, 1), 0], k.rstd[:, bass.ds(i, 1)],
                          ALU.subtract, ALU.mult).then_inc(done.sem, 1)


def flat(t):
    return t.rearrange("p t d -> p (t d)")


def quantized_feed_forward(nc, k, w_gate, w_up, w_down, wo_bias):
    GU = 2 * INNER
    with ExitStack() as ctx:
        w_rows = sbuf(ctx, nc, "w_rows", [P, 6, D])
        wq_rows = sbuf(ctx, nc, "wq_rows", [P, 6, D])
        wd_rows = sbuf(ctx, nc, "wd_rows", [P, INNER])
        wdq_rows = sbuf(ctx, nc, "wdq_rows", [P, INNER])
        bias_b = sbuf(ctx, nc, "bias_b", [P, D])
        wguT = sbuf(ctx, nc, "wguT", [P, GU])
        wdT = sbuf(ctx, nc, "wdT", [P, 3, D])
        HN = TC * INNER
        tmp = [sbuf(ctx, nc, f"fp4_tmp{i}", [P, HN]) for i in range(4)]
        small = [sbuf(ctx, nc, f"fp4_small{i}", [P, HN // QB]) for i in range(3)]
        xn = sbuf(ctx, nc, "xn", [P, TC, D])
        xq = sbuf(ctx, nc, "xq", [P, CH])
        xqT = sbuf(ctx, nc, "xqT", [P, CH])
        silu = sbuf(ctx, nc, "silu_gate", [P, 2, INNER])
        h = sbuf(ctx, nc, "h", [P, TC, INNER])
        hq = sbuf(ctx, nc, "hq", [P, TC, INNER])
        hqT = sbuf(ctx, nc, "hqT", [P, 2, 3, D])
        bank = [psum(ctx, nc, f"ffn_bank{i}", [P, CH]) for i in range(8)]

        def scratch(n):
            return [t[:, 0:n // QB] for t in small] + [t[:, 0:n] for t in tmp]

        loaded = Count(ctx, nc, "ffn_loaded")
        cleared = Count(ctx, nc, "ffn_cleared")
        wlinks = Count(ctx, nc, "ffn_weight_links")
        wturned = Count(ctx, nc, "ffn_weight_turned")
        wkept = Count(ctx, nc, "ffn_weight_kept")
        with nc.Block() as block:
            @block.sync
            def _(sp):
                for i, w in enumerate((w_gate, w_up)):
                    sp.dma_start(w_rows[:, 3 * i:3 * i + 2, :],
                                 w[0:2 * P, :].rearrange("(t p) d -> p t d", p=P)).then_inc(loaded.sem, 16)
                    sp.dma_start(w_rows[0:96, 3 * i + 2, :], w[2 * P:INNER, :]).then_inc(loaded.sem, 16)
                sp.dma_start(wd_rows[:], w_down).then_inc(loaded.sem, 16)
                sp.dma_start(bias_b[:], wo_bias.rearrange("(a d) -> a d", a=1).broadcast_to([P, D]))\
                  .then_inc(loaded.sem, 16)

            @block.vector
            def _(dve):
                dve.memset(w_rows[96:P, 2, :], 0.0).then_inc(cleared.sem, 1)
                dve.memset(w_rows[96:P, 5, :], 0.0).then_inc(cleared.sem, 1)
                dve.wait_ge(cleared.sem, 2)
                dve.wait_ge(loaded.sem, 96)
                chain = Chain(dve, wlinks)
                n = 6 * D
                fp4_round_trip(dve, chain, w_rows[:].rearrange("p t d -> p (t d)"),
                               wq_rows[:].rearrange("p t d -> p (t d)"), *scratch(n), n // QB)
                fp4_round_trip(dve, chain, wd_rows[:], wdq_rows[:], *scratch(INNER), INNER // QB)

            @block.tensor
            def _(pe):
                pe.wait_ge(wlinks.sem, FP4_LINKS)
                for j in range(6):
                    pe.transpose(bank[j // 3][:, j % 3 * P:(j % 3 + 1) * P], wq_rows[:, j, :], k.ident[:])\
                      .then_inc(wturned.sem, 1)
                pe.wait_ge(wlinks.sem, 2 * FP4_LINKS)
                for j, (at, w) in enumerate(IC):
                    pe.transpose(bank[2][0:w, j * P:(j + 1) * P], wdq_rows[:, at:at + w], k.ident[:])\
                      .then_inc(wturned.sem, 1)

            @block.scalar
            def _(act):
                for i in range(2):
                    act.wait_ge(wturned.sem, 3 * i + 3)
                    act.activation(wguT[:, i * INNER:(i + 1) * INNER], bank[i][:, 0:INNER], ACT.Copy)
                act.wait_ge(wturned.sem, 9)
                for j, (at, w) in enumerate(IC):
                    act.activation(wdT[0:w, j, :], bank[2][0:w, j * P:(j + 1) * P], ACT.Copy)


        normed = Count(ctx, nc, "x_normed", TC)
        turned = Count(ctx, nc, "x_turned", 1)
        hi_kept = Count(ctx, nc, "x_hi_kept", 1, credit=1)
        lo_kept = Count(ctx, nc, "x_lo_kept", 1, credit=1)
        links = Count(ctx, nc, "ffn_links", 2 * FP4_LINKS)
        xq_turned = Count(ctx, nc, "xq_turned", 1)
        xq_kept = Count(ctx, nc, "xq_kept", 1, credit=1)
        gated = Count(ctx, nc, "gate_up_ready", TC)
        silu_done = Count(ctx, nc, "silu_ready", TC)
        h_done = Count(ctx, nc, "h_ready", TC, credit=2)
        hq_turned = Count(ctx, nc, "hq_turned", TC)
        hq_kept = Count(ctx, nc, "hq_kept", TC, credit=1)
        downed = Count(ctx, nc, "down_ready", TC)
        added = Count(ctx, nc, "ffn_added", 1, credit=1)
        GATE, UP, HT, DOWN = 2, 4, 6, 7
        def down(pe, c, t):
            for j, (at, w) in enumerate(IC):
                ins = pe.matmul(bank[DOWN][:, t * P:(t + 1) * P], hqT[0:w, t % 2, j, :], wdT[0:w, j, :],
                                start=(j == 0), stop=(j == 2))
            ins.then_inc(downed.sem, 1)

        with nc.Block() as block:
            @block.tensor
            def _(pe):
                with pe.Fori(0, CHUNKS) as c:
                    pe.wait_ge(normed.sem, normed.at(c, TC))
                    pe.wait_ge(hi_kept.sem, hi_kept.at(c, 0))
                    pe.wait_ge(lo_kept.sem, lo_kept.at(c, 0))
                    for t in range(TC):
                        ins = pe.transpose(bank[0][:, t * P:(t + 1) * P], xn[:, t, :], k.ident[:])
                    ins.then_inc(turned.sem, 1)
                    pe.wait_ge(links.sem, links.at(c, FP4_LINKS))
                    pe.wait_ge(xq_kept.sem, xq_kept.at(c, 0))
                    for t in range(TC):
                        ins = pe.transpose(bank[1][:, t * P:(t + 1) * P], xq[:, t * P:(t + 1) * P], k.ident[:])
                    ins.then_inc(xq_turned.sem, 1)
                    pe.wait_ge(xq_kept.sem, xq_kept.at(c, 1))
                    for t in range(TC):
                        pe.wait_ge(h_done.sem, h_done.at(c, t - 1))
                        for b, at in ((GATE, 0), (UP, INNER)):
                            ins = pe.matmul(bank[b + t % 2][:, 0:INNER], xqT[:, t * P:(t + 1) * P],
                                            wguT[:, at:at + INNER], start=True, stop=True)
                        ins.then_inc(gated.sem, 1)
                    pe.wait_ge(links.sem, links.at(c, 2 * FP4_LINKS))
                    pe.wait_ge(added.sem, added.at(c, 0))
                    for t in range(TC):
                        pe.wait_ge(hq_kept.sem, hq_kept.at(c, t))
                        for j, (at, w) in enumerate(IC):
                            ins = pe.transpose(bank[HT][0:w, j * P:(j + 1) * P], hq[:, t, at:at + w], k.ident[:])
                        ins.then_inc(hq_turned.sem, 1)
                        if t:
                            down(pe, c, t - 1)
                    pe.wait_ge(hq_kept.sem, hq_kept.at(c, TC))
                    down(pe, c, TC - 1)

            @block.scalar
            def _(act):
                with act.Fori(0, CHUNKS) as c:
                    act.wait_ge(turned.sem, turned.at(c, 1))
                    act.sem_inc(k.passed, 1)
                    act.activation(k.x_hi[:, bass.ds(c * CH, CH)], bank[0][:], ACT.Copy).then_inc(hi_kept.sem, 1)
                    act.wait_ge(xq_turned.sem, xq_turned.at(c, 1))
                    act.activation(xqT[:], bank[1][:], ACT.Copy).then_inc(xq_kept.sem, 1)
                    for t in range(TC):
                        act.wait_ge(gated.sem, gated.at(c, t + 1))
                        act.activation(silu[:, t % 2, :], bank[GATE + t % 2][:, 0:INNER], ACT.Silu)\
                           .then_inc(silu_done.sem, 1)
                    for t in range(TC):
                        act.wait_ge(hq_turned.sem, hq_turned.at(c, t + 1))
                        if t >= 2:
                            act.wait_ge(downed.sem, downed.at(c, t - 1))
                        act.activation(hqT[:, t % 2, 0:2, :].rearrange("p a d -> p (a d)"),
                                       bank[HT][:, 0:2 * P], ACT.Copy)
                        act.activation(hqT[0:96, t % 2, 2, :], bank[HT][0:96, 2 * P:3 * P], ACT.Copy)\
                           .then_inc(hq_kept.sem, 1)

            @block.vector
            def _(dve):
                with dve.Fori(0, CHUNKS) as c:
                    normalise_chunk(dve, k, c, xn, normed)
                    dve.wait_ge(normed.sem, normed.at(c, TC))
                    chain = Chain(dve, links, c)
                    fp4_round_trip(dve, chain, flat(xn[:]), xq[:], *scratch(CH), CH // QB)
                    dve.wait_ge(hi_kept.sem, hi_kept.at(c, 1))
                    dve.tensor_tensor(k.x_lo[:, bass.ds(c * CH, CH)], bank[0][:],
                                      k.x_hi[:, bass.ds(c * CH, CH)].bitcast(F32), ALU.subtract).then_inc(lo_kept.sem, 1)
                    for t in range(TC):
                        dve.wait_ge(silu_done.sem, silu_done.at(c, t + 1))
                        dve.tensor_tensor(h[:, t, :], bank[UP + t % 2][:, 0:INNER], silu[:, t % 2, :],
                                          ALU.mult).then_inc(h_done.sem, 1)
                    dve.wait_ge(h_done.sem, h_done.at(c, TC))
                    fp4_round_trip(dve, chain, flat(h[:]), flat(hq[:]), *scratch(HN), HN // QB)
                    dve.wait_ge(downed.sem, downed.at(c, TC))
                    out = k.resid[:, bass.ds(c * TC, TC), :]
                    dve.tensor_tensor(flat(out), flat(out), bank[DOWN][:], ALU.add).then_inc(added.sem, 1)
                dve.wait_ge(added.sem, added.at(CHUNKS, 0))
                dve.tensor_tensor(k.resid[:], k.resid[:],
                                  bias_b[:].unsqueeze(1).broadcast_to([P, TILES, D]), ALU.add)

            @block.gpsimd
            def _(pool):
                for count in (hi_kept, lo_kept, xq_kept, h_done, hq_kept, added):
                    pool.sem_inc(count.sem, count.credit)


def attention(nc, k, wqkv, bqk, bv, wo, ghost):
    QK = 4 * P
    with ExitStack() as ctx:
        w_raw = sbuf(ctx, nc, "w_raw", [P, PAIRS, QK + P])
        w_hi = sbuf(ctx, nc, "w_hi", [P, QK + P], F32R)
        w_lo = sbuf(ctx, nc, "w_lo", [P, QK + P], F32R)
        bqk_sb = sbuf(ctx, nc, "bqk_sb", [P, PAIRS, 4])
        bias_now = sbuf(ctx, nc, "bias_now", [P, 4])
        bv_b = sbuf(ctx, nc, "bv_b", [P, PAIRS, P])
        wo_sb = sbuf(ctx, nc, "wo_sb", [P, PAIRS, D])
        ghost_b = sbuf(ctx, nc, "ghost_b", [P, PAIRS, 2])
        xb_hi = sbuf(ctx, nc, "xb_hi", [P, SEQ], F32R)
        xb_lo = sbuf(ctx, nc, "xb_lo", [P, SEQ], F32R)
        q_s = sbuf(ctx, nc, "q_stacked", [P, 2, SEQ], F32R)
        k_hi = sbuf(ctx, nc, "k_high", [P, 2, SEQ], F32R)
        k_lo = sbuf(ctx, nc, "k_low", [P, 2, SEQ], F32R)
        v_sb = sbuf(ctx, nc, "v_sb", [P, TB, P])
        prob = sbuf(ctx, nc, "prob", [P, 2, SEQ])
        probT = [[sbuf(ctx, nc, f"probT{h}{g}", [P, 4 * (g + 1), CH]) for g in range(2)] for h in range(2)]
        negmax = sbuf(ctx, nc, "negmax", [P, 2, TB])
        den = sbuf(ctx, nc, "den", [P, 2, TB])
        rden = sbuf(ctx, nc, "rden", [P, 2, TB])
        av_raw = sbuf(ctx, nc, "av_raw", [P, CH])
        av_sb = sbuf(ctx, nc, "av_sb", [P, CH])
        score = psum(ctx, nc, "score", [P, 2, SEQ])
        turn_bank = psum(ctx, nc, "turn_bank", [P, 2, CH])
        av = psum(ctx, nc, "av", [P, CH])
        rb = psum(ctx, nc, "rb", [P, CH])
        fresh = score[:].rearrange("p a (b n) -> p (a b) n", n=CH)

        loaded = Count(ctx, nc, "attn_loaded")
        scaled = Count(ctx, nc, "bq_scaled")
        bias_in = Count(ctx, nc, "bias_in", 1)
        xb_kept = Count(ctx, nc, "xb_kept", 2)
        w_split = Count(ctx, nc, "w_hi_split", 2)
        w_rest = Count(ctx, nc, "w_lo_split", 2)
        proj = Count(ctx, nc, "qk_projected", 8, credit=1)
        hi_out = Count(ctx, nc, "qk_hi_out", 8)
        lo_out = Count(ctx, nc, "qk_lo_out", 8, credit=4)
        v_proj = Count(ctx, nc, "v_projected", 2, credit=2)
        v_out = Count(ctx, nc, "v_out", 2)
        scored = Count(ctx, nc, "scored", 2 * TB)
        maxed = Count(ctx, nc, "maxed", 2 * TB)
        exped = Count(ctx, nc, "exped", 2 * TB, credit=1)
        turned = Count(ctx, nc, "prob_turned", 24, credit=1)
        kept_act = Count(ctx, nc, "probT_kept_by_act", 12, credit=1)
        kept_dve = Count(ctx, nc, "probT_kept_by_dve", 12, credit=1)
        summed = Count(ctx, nc, "av_ready", 2)
        r_links = Count(ctx, nc, "rden_links", 4)
        spread = Count(ctx, nc, "rden_spread", 2)
        av_out = Count(ctx, nc, "av_out", 2)
        av_done = Count(ctx, nc, "av_normalised", 2)
        outed = Count(ctx, nc, "wo_ready", 2, credit=1)
        added = Count(ctx, nc, "attn_added", 2, credit=1)

        def chunks(i):
            return [(b, min(b + TC, i + 1)) for b in range(0, i + 1, TC)]

        order, e = {}, 0
        for i in range(TB):
            for hd in range(2):
                for c in range(len(chunks(i))):
                    order[i, hd, c] = e
                    e += 1
        assert e == 24
        group_end = [order[3, 1, 0] + 1, 24]

        def keep_turned(eng, mine, count, turn, i, hd, copy):
            for c, (b0, b1) in enumerate(chunks(i)):
                e = order[i, hd, c]
                if e % 2 != mine:
                    continue
                eng.wait_ge(turned.sem, turned.at(turn, e + 1))
                n = b1 - b0
                at = i % TC * P
                copy(probT[hd][i // TC][:, b0:b1, at:at + P],
                     turn_bank[:, e % 2, 0:n * P].rearrange("p (b n) -> p b n", n=P)).then_inc(count.sem, 1)

        block = ctx.enter_context(nc.Block())

        @block.sync
        def _(sp):
            sp.dma_start(w_raw[:], wqkv.rearrange("a k m -> k a m")).then_inc(loaded.sem, 16)
            sp.dma_start(bqk_sb[:], bqk.rearrange("a p m -> p a m")).then_inc(loaded.sem, 16)
            sp.dma_start(bv_b[:].rearrange("p a m -> p (a m)"),
                         bv.rearrange("(a n) -> a n", a=1).broadcast_to([P, HEADS * DH])).then_inc(loaded.sem, 16)
            sp.dma_start(wo_sb[:], wo.rearrange("(a p) m -> p a m", p=P)).then_inc(loaded.sem, 16)
            sp.dma_start(ghost_b[:].rearrange("p a m -> p (a m)"),
                         ghost.rearrange("(a n) -> a n", a=1).broadcast_to([P, HEADS])).then_inc(loaded.sem, 16)

        @block.gpsimd
        def _(pool):
            for count in (proj, lo_out, v_proj, exped, turned, kept_act, kept_dve, outed, added):
                pool.sem_inc(count.sem, count.credit)

        @block.tensor
        def _(pe):
            with pe.Fori(0, BATCH) as b:
                with pe.Fori(0, PAIRS) as p:
                    turn = b * PAIRS + p
                    pe.wait_ge(w_split.sem, w_split.at(turn, 2))
                    pe.wait_ge(w_rest.sem, w_rest.at(turn, 2))
                    pe.wait_ge(xb_kept.sem, xb_kept.at(b, 2))
                    pe.wait_ge(exped.sem, exped.at(turn, 0))
                    for n in range(8):
                        pe.wait_ge(lo_out.sem, lo_out.at(turn, n - 3))
                        w = slice(n // 2 * P, n // 2 * P + P)
                        x = slice(n % 2 * CH, n % 2 * CH + CH)
                        pe.matmul(fresh[:, n % 4, :], w_hi[:, w], xb_hi[:, x], start=True, stop=False)
                        pe.matmul(fresh[:, n % 4, :], w_hi[:, w], xb_lo[:, x], start=False, stop=False)
                        pe.matmul(fresh[:, n % 4, :], w_lo[:, w], xb_hi[:, x], start=False, stop=True)\
                          .then_inc(proj.sem, 1)
                    pe.wait_ge(kept_act.sem, kept_act.at(turn, 0))
                    pe.wait_ge(kept_dve.sem, kept_dve.at(turn, 0))
                    for t in range(TB):
                        to = turn_bank[:, t // TC, t % TC * P:t % TC * P + P]
                        x = slice(t * P, t * P + P)
                        pe.matmul(to, xb_hi[:, x], w_hi[:, QK:], start=True, stop=False)
                        pe.matmul(to, xb_hi[:, x], w_lo[:, QK:], start=False, stop=False)
                        ins = pe.matmul(to, xb_lo[:, x], w_hi[:, QK:], start=False, stop=True)
                        if t % TC == TC - 1:
                            ins.then_inc(v_proj.sem, 1)

                    def scores(i, hd):
                        q = q_s[:, hd, i * P:i * P + P]
                        width = (i + 1) * P
                        for c0 in range(0, width, CH):
                            c1 = min(c0 + CH, width)
                            last = c1 == width
                            pe.matmul(score[:, hd, c0:c1], q, k_hi[:, hd, c0:c1], start=True, stop=False)
                            ins = pe.matmul(score[:, hd, c0:c1], q, k_lo[:, hd, c0:c1], start=False,
                                            stop=not last)
                        ins = pe.matmul(score[:, hd, i * P:width], k.identb[:], k.maskb[:], start=False, stop=True)
                        ins.then_inc(scored.sem, 1)

                    def turns(i, hd):
                        for c, (b0, b1) in enumerate(chunks(i)):
                            e = order[i, hd, c]
                            count = kept_dve if e % 2 else kept_act
                            pe.wait_ge(count.sem, count.at(turn, e // 2))
                            for blk in range(b0, b1):
                                ins = pe.transpose(turn_bank[:, e % 2, (blk - b0) * P:(blk - b0 + 1) * P],
                                                   prob[:, hd, blk * P:(blk + 1) * P], k.ident[:])
                            ins.then_inc(turned.sem, 1)

                    def values(g):
                        pe.wait_ge(kept_act.sem, kept_act.at(turn, group_end[g] // 2))
                        pe.wait_ge(kept_dve.sem, kept_dve.at(turn, group_end[g] // 2))
                        pe.wait_ge(added.sem, added.at(turn, g))
                        nb = TC * (g + 1)
                        for blk in range(nb):
                            c0 = max(blk - TC * g, 0) * P
                            for hd in range(2):
                                r = slice(hd * DH, hd * DH + DH)
                                ins = pe.matmul(av[r, c0:CH], v_sb[:, blk, r], probT[hd][g][:, blk, c0:CH],
                                                start=(blk == 0), stop=(blk == nb - 1))
                        ins.then_inc(summed.sem, 1)
                        pe.wait_ge(r_links.sem, r_links.at(turn, 2 * g + 2))
                        for t in range(TC):
                            for hd in range(2):
                                i = g * TC + t
                                ins = pe.matmul(rb[hd * DH:(hd + 1) * DH, t * P:(t + 1) * P],
                                                rden[:, hd, i:i + 1].broadcast_to([P, DH]), k.ident[:],
                                                start=True, stop=True)
                        ins.then_inc(spread.sem, 1)

                    def output(g):
                        pe.wait_ge(av_done.sem, av_done.at(turn, g + 1))
                        for t in range(TC):
                            ins = pe.matmul(av[:, t * P:(t + 1) * P], av_sb[:, t * P:(t + 1) * P],
                                            wo_sb[:, bass.ds(p, 1), :].rearrange("p a d -> p (a d)"),
                                            start=True, stop=True)
                        ins.then_inc(outed.sem, 1)

                    pe.wait_ge(lo_out.sem, lo_out.at(turn, 8))
                    scores(0, 0)
                    scores(0, 1)
                    pe.wait_ge(v_out.sem, v_out.at(turn, 2))
                    for i in range(TB):
                        for hd in range(2):
                            pe.wait_ge(exped.sem, exped.at(turn, 2 * i + hd + 1))
                            turns(i, hd)
                            if i + 1 < TB:
                                scores(i + 1, hd)
                        if i == 4:
                            values(0)
                        if i == 5:
                            output(0)
                    values(1)
                    output(1)

        @block.scalar
        def _(act):
            act.wait_ge(loaded.sem, 80)
            act.wait_ge(scaled.sem, 1)
            act.sem_inc(k.passed, 1)
            with act.Fori(0, BATCH) as b:
                act.wait_ge(v_proj.sem, v_proj.at(b * PAIRS, 0))
                act.sem_inc(k.passed, 1)
                act.activation(xb_hi[:], k.x_hi[:, bass.ds(b * SEQ, SEQ)].bitcast(F32), ACT.Copy)\
                   .then_inc(xb_kept.sem, 1)
                act.activation(xb_lo[:], k.x_lo[:, bass.ds(b * SEQ, SEQ)].bitcast(F32), ACT.Copy)\
                   .then_inc(xb_kept.sem, 1)
                with act.Fori(0, PAIRS) as p:
                    turn = b * PAIRS + p
                    act.wait_ge(v_proj.sem, v_proj.at(turn, 0))
                    act.sem_inc(k.passed, 1)
                    act.wait_ge(lo_out.sem, lo_out.at(turn, 0))
                    act.sem_inc(k.passed, 1)
                    act.activation(bias_now[:], bqk_sb[:, bass.ds(p, 1), :].rearrange("p a m -> p (a m)"), ACT.Copy)\
                       .then_inc(bias_in.sem, 1)
                    act.wait_ge(bias_in.sem, bias_in.at(turn, 1))
                    act.sem_inc(k.passed, 1)
                    w = w_raw[:, bass.ds(p, 1), :].rearrange("p a m -> p (a m)")
                    act.activation(w_hi[:, 0:2 * P], w[:, 0:2 * P], ACT.Copy, scale=DH ** -0.5)\
                       .then_inc(w_split.sem, 1)
                    act.activation(w_hi[:, 2 * P:], w[:, 2 * P:], ACT.Copy).then_inc(w_split.sem, 1)
                    for n in range(8):
                        act.wait_ge(proj.sem, proj.at(turn, n + 1))
                        to = (q_s if n < 4 else k_hi)[:, n // 2 % 2, n % 2 * CH:n % 2 * CH + CH]
                        act.activation(to, fresh[:, n % 4, :], ACT.Identity,
                                       bias=bias_now[:, n // 2:n // 2 + 1]).then_inc(hi_out.sem, 1)

                    def exps(i, hd):
                        act.wait_ge(maxed.sem, maxed.at(turn, 2 * i + hd + 1))
                        if i:
                            act.wait_ge(turned.sem, turned.at(turn, order[i - 1, hd, len(chunks(i - 1)) - 1] + 1))
                        else:
                            act.wait_ge(turned.sem, turned.at(turn, 0))
                        act.activation(prob[:, hd, 0:(i + 1) * P], score[:, hd, 0:(i + 1) * P], ACT.Exp,
                                       bias=negmax[:, hd, i:i + 1], accum_out=den[:, hd, i:i + 1])\
                           .then_inc(exped.sem, 1)

                    def av_copy(g):
                        act.wait_ge(summed.sem, summed.at(turn, g + 1))
                        act.activation(av_raw[:], av[:], ACT.Copy).then_inc(av_out.sem, 1)

                    copy = lambda out, in_: act.activation(out, in_, ACT.Copy)
                    exps(0, 0)
                    exps(0, 1)
                    for i in range(TB):
                        for hd in range(2):
                            keep_turned(act, 0, kept_act, turn, i, hd, copy)
                            if i + 1 < TB:
                                exps(i + 1, hd)
                        if i == 4:
                            av_copy(0)
                    av_copy(1)

        @block.vector
        def _(dve):
            dve.wait_ge(loaded.sem, 80)
            dve.tensor_scalar(bqk_sb[:, :, 0:2], bqk_sb[:, :, 0:2], DH ** -0.5, None, ALU.mult)\
               .then_inc(scaled.sem, 1)
            with dve.Fori(0, BATCH) as b:
                with dve.Fori(0, PAIRS) as p:
                    turn = b * PAIRS + p
                    w = w_raw[:, bass.ds(p, 1), :].rearrange("p a m -> p (a m)")
                    dve.wait_ge(w_split.sem, w_split.at(turn, 2))
                    dve.scalar_tensor_tensor(out=w_lo[:, 0:2 * P], in0=w[:, 0:2 * P], scalar=DH ** -0.5,
                                             in1=w_hi[:, 0:2 * P].bitcast(F32), op0=ALU.mult, op1=ALU.subtract)\
                       .then_inc(w_rest.sem, 1)
                    dve.tensor_tensor(w_lo[:, 2 * P:], w[:, 2 * P:], w_hi[:, 2 * P:].bitcast(F32), ALU.subtract)\
                       .then_inc(w_rest.sem, 1)
                    for n in range(8):
                        dve.wait_ge(hi_out.sem, hi_out.at(turn, n + 1))
                        hd, cols = n // 2 % 2, slice(n % 2 * CH, n % 2 * CH + CH)
                        bias = bias_now[:, n // 2:n // 2 + 1]
                        if n < 4:
                            low = slice(DH, P)
                            dve.scalar_tensor_tensor(out=q_s[low, hd, cols], in0=fresh[low, n % 4, :],
                                                     scalar=bias[low], in1=q_s[low, hd, cols].bitcast(F32),
                                                     op0=ALU.add, op1=ALU.subtract).then_inc(lo_out.sem, 1)
                        else:
                            dve.scalar_tensor_tensor(out=k_lo[:, hd, cols], in0=fresh[:, n % 4, :],
                                                     scalar=bias, in1=k_hi[:, hd, cols].bitcast(F32),
                                                     op0=ALU.add, op1=ALU.subtract).then_inc(lo_out.sem, 1)
                    for u in range(2):
                        dve.wait_ge(v_proj.sem, v_proj.at(turn, u + 1))
                        dve.tensor_tensor(v_sb[:, u * TC:(u + 1) * TC, :],
                                          turn_bank[:, u, :].rearrange("p (t m) -> p t m", m=P),
                                          bv_b[:, bass.ds(p, 1), :].broadcast_to([P, TC, P]), ALU.add)\
                           .then_inc(v_out.sem, 1)

                    def maxes(i, hd):
                        dve.wait_ge(scored.sem, scored.at(turn, 2 * i + hd + 1))
                        dve.tensor_reduce(negmax[:, hd, i:i + 1], score[:, hd, 0:(i + 1) * P], AX.X, ALU.max,
                                          negate=True).then_inc(maxed.sem, 1)

                    def rdens(g):
                        dve.wait_ge(exped.sem, exped.at(turn, 8 * g + 8))
                        t = slice(g * TC, g * TC + TC)
                        dve.tensor_tensor(den[:, :, t], den[:, :, t],
                                          ghost_b[:, bass.ds(p, 1), :].rearrange("p a h -> p h a")
                                          .broadcast_to([P, 2, TC]), ALU.add).then_inc(r_links.sem, 1)
                        dve.wait_ge(r_links.sem, r_links.at(turn, 2 * g + 1))
                        dve.reciprocal(rden[:, :, t], den[:, :, t]).then_inc(r_links.sem, 1)

                    def normalised(g):
                        dve.wait_ge(spread.sem, spread.at(turn, g + 1))
                        dve.wait_ge(av_out.sem, av_out.at(turn, g + 1))
                        dve.wait_ge(outed.sem, outed.at(turn, g))
                        dve.tensor_tensor(av_sb[:], rb[:], av_raw[:], ALU.mult).then_inc(av_done.sem, 1)

                    def add_out(g):
                        dve.wait_ge(outed.sem, outed.at(turn, g + 1))
                        out = k.resid[:, bass.ds(b * TB + g * TC, TC), :]
                        dve.tensor_tensor(flat(out), flat(out), av[:], ALU.add).then_inc(added.sem, 1)

                    copy = lambda out, in_: dve.tensor_copy(out, in_)
                    maxes(0, 0)
                    maxes(0, 1)
                    for i in range(TB):
                        for hd in range(2):
                            keep_turned(dve, 1, kept_dve, turn, i, hd, copy)
                            if i + 1 < TB:
                                maxes(i + 1, hd)
                        if i == 3:
                            rdens(0)
                        if i == 4:
                            normalised(0)
                        if i == 5:
                            add_out(0)
                    rdens(1)
                    normalised(1)
                    add_out(1)


def second_norm_and_routing(nc, k, router_w, router_b, gates_dram):
    with ExitStack() as ctx:
        xn = sbuf(ctx, nc, "xn2", [P, TC, D])
        rw = sbuf(ctx, nc, "router_w_sb", [P, EXPERTS])
        rbias = sbuf(ctx, nc, "router_b_sb", [EXPERTS, 1])
        logT = sbuf(ctx, nc, "logits_t", [EXPERTS, CH])
        logits = sbuf(ctx, nc, "logits", [P, TILES, EXPERTS])
        best = sbuf(ctx, nc, "best", [P, TILES, 8])
        which = sbuf(ctx, nc, "which", [P, TILES, 8], U32)
        whichf = sbuf(ctx, nc, "which_f", [P, TILES, 2])
        number = sbuf(ctx, nc, "expert_number", [P, EXPERTS])
        gap = sbuf(ctx, nc, "gap", [P, TILES])
        second = sbuf(ctx, nc, "second", [P, TILES])
        gate = sbuf(ctx, nc, "gate", [P, 2, TILES])
        hit = [sbuf(ctx, nc, f"hit{i}", [P, TILES, EXPERTS]) for i in range(2)]
        gatesT = sbuf(ctx, nc, "gates_t", [EXPERTS, BATCH * SEQ])
        bank = [psum(ctx, nc, f"route_bank{i}", [P, CH]) for i in range(8)]

        loaded = Count(ctx, nc, "route_loaded")
        normed = Count(ctx, nc, "x2_normed", TC)
        turned = Count(ctx, nc, "x2_turned", 1, credit=1)
        state_out = Count(ctx, nc, "state_kept", 1)
        hi_out = Count(ctx, nc, "x2_hi_kept", 1, credit=1)
        lo_out = Count(ctx, nc, "x2_lo_kept", 1, credit=1)
        logit = Count(ctx, nc, "logits_ready", 1)
        log_out = Count(ctx, nc, "logits_biased", 1)
        log_turned = Count(ctx, nc, "logits_turned", 1)
        log_kept = Count(ctx, nc, "logits_kept", 1, credit=1)
        with nc.Block() as block:
            @block.sync
            def _(sp):
                sp.dma_start(rw[:], router_w).then_inc(loaded.sem, 16)
                sp.dma_start(rbias[:], router_b.rearrange("(e a) -> e a", a=1)).then_inc(loaded.sem, 16)

            @block.gpsimd
            def _(pool):
                for count in (turned, hi_out, lo_out, log_kept):
                    pool.sem_inc(count.sem, count.credit)

            @block.tensor
            def _(pe):
                pe.wait_ge(loaded.sem, 32)
                with pe.Fori(0, CHUNKS) as c:
                    pe.wait_ge(normed.sem, normed.at(c, TC))
                    pe.wait_ge(lo_out.sem, lo_out.at(c, 0))
                    for t in range(TC):
                        ins = pe.transpose(bank[0][:, t * P:(t + 1) * P], xn[:, t, :], k.ident[:])
                    ins.then_inc(turned.sem, 1)
                    pe.wait_ge(state_out.sem, state_out.at(c, 1))
                    pe.matmul(bank[1][0:EXPERTS, :], rw[:], k.state[:, bass.ds(c * CH, CH)], start=True, stop=True)\
                      .then_inc(logit.sem, 1)
                    pe.wait_ge(log_out.sem, log_out.at(c, 1))
                    pe.wait_ge(log_kept.sem, log_kept.at(c, 0))
                    pe.sem_inc(k.passed, 1)
                    for t in range(TC):
                        ins = pe.transpose(bank[2][:, t * EXPERTS:(t + 1) * EXPERTS], logT[:, t * P:(t + 1) * P],
                                           k.ident[0:EXPERTS, 0:EXPERTS])
                    ins.then_inc(log_turned.sem, 1)

            @block.scalar
            def _(act):
                act.wait_ge(loaded.sem, 32)
                with act.Fori(0, CHUNKS) as c:
                    act.wait_ge(turned.sem, turned.at(c, 1))
                    act.sem_inc(k.passed, 1)
                    cols = bass.ds(c * CH, CH)
                    act.activation(k.state[:, cols], bank[0][:], ACT.Copy).then_inc(state_out.sem, 1)
                    act.activation(k.x_hi[:, cols], bank[0][:], ACT.Copy).then_inc(hi_out.sem, 1)
                    act.wait_ge(logit.sem, logit.at(c, 1))
                    act.activation(logT[:], bank[1][0:EXPERTS, :], ACT.Identity, bias=rbias[:])\
                       .then_inc(log_out.sem, 1)

            @block.vector
            def _(dve):
                with dve.Fori(0, CHUNKS) as c:
                    dve.wait_ge(turned.sem, turned.at(c, 0))
                    normalise_chunk(dve, k, c, xn, normed)
                    dve.wait_ge(hi_out.sem, hi_out.at(c, 1))
                    dve.tensor_tensor(k.x_lo[:, bass.ds(c * CH, CH)], bank[0][:],
                                      k.x_hi[:, bass.ds(c * CH, CH)].bitcast(F32), ALU.subtract)\
                       .then_inc(lo_out.sem, 1)
                    dve.wait_ge(log_turned.sem, log_turned.at(c, 1))
                    dve.tensor_copy(flat(logits[:, bass.ds(c * TC, TC), :]), bank[2][:, 0:TC * EXPERTS])\
                       .then_inc(log_kept.sem, 1)

        numbered = Count(ctx, nc, "experts_numbered")
        found = Count(ctx, nc, "best_found")
        links = Count(ctx, nc, "gate_links")
        exped = Count(ctx, nc, "second_exped")
        gturned = Count(ctx, nc, "gates_turned")
        gkept = Count(ctx, nc, "gates_kept")
        stored = Count(ctx, nc, "gates_stored")
        with nc.Block() as block:
            @block.gpsimd
            def _(pool):
                for e in range(EXPERTS):
                    ins = pool.memset(number[:, e:e + 1], float(e))
                    ins.then_inc(numbered.sem, 1)

            @block.vector
            def _(dve):
                for t in range(TILES):
                    dve.max(best[:, t, :], logits[:, t, :]).then_inc(found.sem, 1)
                dve.wait_ge(found.sem, TILES)
                for t in range(TILES):
                    ins = dve.max_index(which[:, t, :], best[:, t, :], logits[:, t, :])
                ins.then_inc(found.sem, 1)
                chain = Chain(dve, links)
                link = chain.link
                link(dve.tensor_tensor(gap[:], best[:, :, 1], best[:, :, 0], ALU.subtract))
                dve.wait_ge(found.sem, TILES + 1)
                link(dve.tensor_copy(whichf[:], which[:, :, 0:2]))
                dve.wait_ge(exped.sem, 1)
                link(dve.tensor_scalar(gap[:], second[:], 1.0, None, ALU.add))
                link(dve.reciprocal(gate[:, 0, :], gap[:]))
                link(dve.tensor_tensor(gate[:, 1, :], second[:], gate[:, 0, :], ALU.mult))
                dve.wait_ge(numbered.sem, EXPERTS)
                shape = [P, TILES, EXPERTS]
                for i in range(2):
                    link(dve.tensor_tensor(hit[i][:], whichf[:, :, i:i + 1].broadcast_to(shape),
                                           number[:].unsqueeze(1).broadcast_to(shape), ALU.is_equal))
                    link(dve.tensor_tensor(hit[i][:], hit[i][:], gate[:, i, :].unsqueeze(2).broadcast_to(shape),
                                           ALU.mult))
                link(dve.tensor_tensor(hit[0][:], hit[0][:], hit[1][:], ALU.add))

            @block.scalar
            def _(act):
                act.wait_ge(links.sem, 1)
                act.activation(second[:], gap[:], ACT.Exp).then_inc(exped.sem, 1)
                for c in range(CHUNKS):
                    act.wait_ge(gturned.sem, c + 1)
                    act.activation(gatesT[:, c * CH:(c + 1) * CH], bank[c][0:EXPERTS, :], ACT.Copy)\
                       .then_inc(gkept.sem, 1)

            @block.tensor
            def _(pe):
                pe.wait_ge(links.sem, 10)
                for c in range(CHUNKS):
                    for t in range(TC):
                        ins = pe.transpose(bank[c][0:EXPERTS, t * P:(t + 1) * P], hit[0][:, c * TC + t, :],
                                           k.ident[:])
                    ins.then_inc(gturned.sem, 1)

            @block.sync
            def _(sp):
                sp.wait_ge(gkept.sem, CHUNKS)
                sp.dma_start(gates_dram, gatesT[:]).then_inc(stored.sem, 16)
                sp.wait_ge(stored.sem, 16)


(BQ, BK, BV, BO, S1, B1N, BF, B2F, S2, B2N) = (0, 1, 2, 3, 4, 5, 6, 10, 11, 12)
COLS = 13


def linear_layers(nc, k, wqkv, wo, w1, w2, columns):
    with ExitStack() as ctx:
        wqkv_sb = [sbuf(ctx, nc, f"l_wqkv{u}", [P, 3, D]) for u in range(2)]
        wo_sb = [sbuf(ctx, nc, f"l_wo{u}", [P, D]) for u in range(2)]
        w1_sb = [sbuf(ctx, nc, f"l_w1{u}", [P, FF]) for u in range(2)]
        w2_sb = [sbuf(ctx, nc, f"l_w2{u}", [P, FC, D]) for u in range(2)]
        col = [sbuf(ctx, nc, f"l_col{u}", [P, COLS]) for u in range(2)]
        plus = [sbuf(ctx, nc, f"l_plus{u}", [P, 2]) for u in range(2)]
        eps_attn = sbuf(ctx, nc, "l_eps_attn", [P, 1])
        power = sbuf(ctx, nc, "l_power", [P, TC])
        ek = sbuf(ctx, nc, "l_ek", [P, 2, CH])
        kf = sbuf(ctx, nc, "l_kf", [P, 2, CH])
        junk = sbuf(ctx, nc, "l_junk", [P, 2, CH])
        eq = sbuf(ctx, nc, "l_eq", [P, 2, CH])
        q = sbuf(ctx, nc, "l_q", [P, CHUNKS, CH])
        yk = sbuf(ctx, nc, "l_yk", [P, 2, CH])
        sums = sbuf(ctx, nc, "l_sums", [P, 2, CHUNKS])
        tot = sbuf(ctx, nc, "l_tot", [P, 2, BATCH])
        ratio = sbuf(ctx, nc, "l_ratio", [P, BATCH])
        inv = sbuf(ctx, nc, "l_inv", [P, BATCH])
        less = sbuf(ctx, nc, "l_less", [P, BATCH])
        att = sbuf(ctx, nc, "l_att", [P, 2, CH])
        ff_out = sbuf(ctx, nc, "l_ff_out", [P, CH])
        x1 = sbuf(ctx, nc, "l_x1", [P, 3, CH])
        h = sbuf(ctx, nc, "l_h", [P, FC, CH])
        y = [sbuf(ctx, nc, f"l_y{s}", [P, 2, CH]) for s in range(2)]
        xhat = [sbuf(ctx, nc, f"l_xhat{s}", [P, 2, CH]) for s in range(2)]
        stats = [sbuf(ctx, nc, f"l_stats{s}", [P, 2, TC, 6]) for s in range(2)]
        mv = [sbuf(ctx, nc, f"l_mv{s}", [P, 2, TC, 2]) for s in range(2)]
        var = [sbuf(ctx, nc, f"l_var{s}", [P, 2, TC]) for s in range(2)]
        rstd = [sbuf(ctx, nc, f"l_rstd{s}", [P, 2, TC]) for s in range(2)]
        bank = [psum(ctx, nc, f"l_bank{i}", [P, CH]) for i in range(8)]

        N = 2 * CHUNKS

        def count(name, per=N, credit=0):
            return Count(ctx, nc, f"l_{name}", per, credit)

        consts = count("consts", 0)
        w_in = [count(f"weights_in{u}", 16 * 5) for u in range(2)]
        plus_in = count("plus", 2)
        kq_m = count("k_ready", N); v_m = count("v_ready", N); q_m = count("q_ready", N)
        ek_a = count("ek", N); eq_a = count("eq", N)
        ekc = count("ek_clipped", N); eqc = count("eq_clipped", N)
        eqr = count("eq_rounded", N)
        k_d = count("k_summed", N, credit=2)
        kv_d = count("kv_summed", N, credit=2)
        q_d = count("q_kept", N, credit=2)
        tiny = count("tiny_links", 2 * BATCH * 5)
        ln_a = count("log_done", N)
        y_a = count("inverse_done", N)
        v_d = count("v_done", N, credit=2)
        wo_m = count("wo_ready", N)
        att_a = count("attn_gelu", N, credit=1)
        add = [count(f"added{s}", N, credit=3) for s in range(2)]
        t_a = [count(f"turned{s}", N, credit=2) for s in range(2)]
        st = [count(f"stats{s}", N * TC) for s in range(2)]
        ag = [count(f"aggregated{s}", N) for s in range(2)]
        ve = [count(f"var_eps{s}", N) for s in range(2)]
        rs = [count(f"rstd{s}", N) for s in range(2)]
        nm = [count(f"normed{s}", N, credit=2) for s in range(2)]
        t_b = [count(f"turned_back{s}", N, credit=2) for s in range(2)]
        out = [count(f"x_out{s}", N, credit=9) for s in range(2)]
        f1 = count("ff1_ready", N * FC)
        hg = count("h_gelu", N * FC, credit=2)
        f2 = count("ff2_ready", N, credit=1)
        g2 = count("ff_gelu", N, credit=1)

        block = ctx.enter_context(nc.Block())
        KB, VB, QBK = 0, 1, 2
        WO, TA, TBK, F1, F2, TA2, TB2 = 0, 1, 2, 3, 5, 6, 7

        credited = (k_d, kv_d, q_d, v_d, att_a, *add, *t_a, *nm, *t_b, *out, hg, f2, g2)

        @block.sync
        def _(sp):
            with sp.Fori(0, LAYERS // 2) as j:
                for u in range(2):
                    sp.wait_ge(out[1].sem, out[1].at(j, (u - 1) * CHUNKS))
                    sp.sem_inc(k.passed, 1)
                    i = j * 2 + u
                    one = bass.ds(i, 1)
                    sp.dma_start(wqkv_sb[u][:], wqkv[one].rearrange("a w k m -> k (a w) m")).then_inc(w_in[u].sem, 16)
                    sp.dma_start(wo_sb[u][:], wo[one].rearrange("a k m -> (a k) m")).then_inc(w_in[u].sem, 16)
                    sp.dma_start(w1_sb[u][:], w1[one].rearrange("a k m -> (a k) m")).then_inc(w_in[u].sem, 16)
                    sp.dma_start(w2_sb[u][:], w2[one].rearrange("a (f k) m -> k (a f) m", k=P)).then_inc(w_in[u].sem, 16)
                    sp.dma_start(col[u][:], columns[one].rearrange("a p c -> (a p) c")).then_inc(w_in[u].sem, 16)

        @block.gpsimd
        def _(pool):
            for c in credited:
                pool.sem_inc(c.sem, c.credit)
            pool.memset(eps_attn[:], EPS_ATTN).then_inc(consts.sem, 1)
            pool.memset(power[:], -0.5).then_inc(consts.sem, 1)
            pool.wait_ge(consts.sem, 2)
            with pool.Fori(0, LAYERS // 2) as j:
                for u in range(2):
                    def inverse_roots(s, c):
                        n, r = u * CHUNKS + c, c % 2
                        pool.wait_ge(ag[s].sem, ag[s].at(j, n + 1))
                        pool.sem_inc(k.passed, 1)
                        pool.tensor_scalar(var[s][:, r, :], mv[s][:, r, :, 1], EPS_LN, None, ALU.add)\
                            .then_inc(ve[s].sem, 1)
                        pool.wait_ge(ve[s].sem, ve[s].at(j, n + 1))
                        pool.wait_ge(nm[s].sem, nm[s].at(j, n - 1))
                        pool.tensor_tensor(rstd[s][:, r, :], var[s][:, r, :], power[:], ALU.pow)\
                            .then_inc(rs[s].sem, 1)
                    for slot in range(CHUNKS + 5):
                        if 0 <= slot - 1 < CHUNKS:
                            inverse_roots(0, slot - 1)
                        if 0 <= slot - 4 < CHUNKS:
                            inverse_roots(1, slot - 4)

        @block.tensor
        def _(pe):
            with pe.Fori(0, LAYERS // 2) as j:
                for u in range(2):
                    pe.wait_ge(w_in[u].sem, w_in[u].at(j, 80))
                    pe.wait_ge(out[1].sem, out[1].at(j, u * CHUNKS))
                    for c in range(CHUNKS):
                        n, base = u * CHUNKS + c, c % 2 * 3
                        for which, count_in, count_out in ((1, k_d, kq_m), (2, kv_d, v_m), (0, q_d, q_m)):
                            pe.wait_ge(count_in.sem, count_in.at(j, n - 1))
                            to = bank[base + {1: KB, 2: VB, 0: QBK}[which]]
                            pe.matmul(to[:], wqkv_sb[u][:, which, :], k.state[:, c * CH:(c + 1) * CH],
                                      start=True, stop=True).then_inc(count_out.sem, 1)
                    for count_in in (k_d, kv_d, q_d):
                        pe.wait_ge(count_in.sem, count_in.at(j, (u + 1) * CHUNKS))

                    def turn(to, src, waits, signal):
                        for c_, v in waits:
                            pe.wait_ge(c_.sem, v)
                        for t in range(TC):
                            ins = pe.transpose(to[:, t * P:(t + 1) * P], src[:, t * P:(t + 1) * P], k.ident[:])
                        ins.then_inc(signal.sem, 1)

                    for slot in range(CHUNKS + 5):
                        c = slot
                        if c < CHUNKS:
                            n = u * CHUNKS + c
                            pe.wait_ge(v_d.sem, v_d.at(j, n + 1))
                            pe.wait_ge(att_a.sem, att_a.at(j, n))
                            pe.matmul(bank[WO][:], wo_sb[u][:], q[:, c, :], start=True, stop=True)\
                              .then_inc(wo_m.sem, 1)
                        c = slot - 1
                        if 0 <= c < CHUNKS:
                            n = u * CHUNKS + c
                            turn(bank[TA], y[0][:, c % 2, :], ((add[0], add[0].at(j, n + 1)), (nm[0], nm[0].at(j, n))),
                                 t_a[0])
                        c = slot - 3
                        if 0 <= c < CHUNKS:
                            n = u * CHUNKS + c
                            pe.wait_ge(out[0].sem, out[0].at(j, n + 1))
                            for f in range(FC):
                                pe.wait_ge(hg.sem, hg.at(j, n * FC + f - 1))
                                pe.matmul(bank[F1 + f % 2][:], w1_sb[u][:, f * P:(f + 1) * P], x1[:, c % 3, :],
                                          start=True, stop=True).then_inc(f1.sem, 1)
                        c = slot - 2
                        if 0 <= c < CHUNKS:
                            n = u * CHUNKS + c
                            turn(bank[TBK], xhat[0][:, c % 2, :],
                                 ((nm[0], nm[0].at(j, n + 1)), (out[0], out[0].at(j, n))), t_b[0])
                        c = slot - 3
                        if 0 <= c < CHUNKS:
                            n = u * CHUNKS + c
                            pe.wait_ge(g2.sem, g2.at(j, n))
                            for f in range(FC):
                                pe.wait_ge(hg.sem, hg.at(j, n * FC + f + 1))
                                ins = pe.matmul(bank[F2][:], w2_sb[u][:, f, :], h[:, f, :],
                                                start=(f == 0), stop=(f == FC - 1))
                            ins.then_inc(f2.sem, 1)
                        c = slot - 4
                        if 0 <= c < CHUNKS:
                            n = u * CHUNKS + c
                            turn(bank[TA2], y[1][:, c % 2, :], ((add[1], add[1].at(j, n + 1)), (nm[1], nm[1].at(j, n))),
                                 t_a[1])
                        c = slot - 5
                        if 0 <= c < CHUNKS:
                            n = u * CHUNKS + c
                            turn(bank[TB2], xhat[1][:, c % 2, :],
                                 ((nm[1], nm[1].at(j, n + 1)), (out[1], out[1].at(j, n))), t_b[1])

        @block.scalar
        def _(act):
            act.wait_ge(consts.sem, 2)
            act.sem_inc(k.passed, 1)
            with act.Fori(0, LAYERS // 2) as j:
                for u in range(2):
                    act.wait_ge(w_in[u].sem, w_in[u].at(j, 80))

                    def one(i):
                        return col[u][:, i:i + 1]

                    for c in range(CHUNKS + 2):
                        if c < CHUNKS:
                            n, r = u * CHUNKS + c, c % 2
                            act.wait_ge(ekc.sem, ekc.at(j, n + 1))
                            act.activation(ek[:, r, :], ek[:, r, :], ACT.Exp).then_inc(ek_a.sem, 1)
                            act.wait_ge(eqc.sem, eqc.at(j, n + 1))
                            act.activation(eq[:, r, :], eq[:, r, :], ACT.Exp).then_inc(eq_a.sem, 1)
                        if c % 2 and c >= 3:
                            b = (c - 3) // 2
                            act.wait_ge(tiny.sem, tiny.at(j, (u * BATCH + b + 1) * 5))
                            for cc in (2 * b, 2 * b + 1):
                                n = u * CHUNKS + cc
                                act.wait_ge(q_d.sem, q_d.at(j, n + 1))
                                act.wait_ge(v_d.sem, v_d.at(j, n - 1))
                                act.activation(yk[:, cc % 2, :], q[:, cc, :], ACT.Ln, bias=eps_attn[:],
                                               scale=tot[:, 0, b:b + 1]).then_inc(ln_a.sem, 1)
                                act.wait_ge(ln_a.sem, ln_a.at(j, n + 1))
                                act.activation(yk[:, cc % 2, :], yk[:, cc % 2, :], ACT.Exp, scale=-1.0)\
                                   .then_inc(y_a.sem, 1)
                    for slot in range(CHUNKS + 5):
                        c = slot
                        if c < CHUNKS:
                            n = u * CHUNKS + c
                            act.wait_ge(wo_m.sem, wo_m.at(j, n + 1))
                            act.wait_ge(add[0].sem, add[0].at(j, n - 1))
                            act.activation(att[:, c % 2, :], bank[WO][:], ACT.Gelu_apprx_tanh, bias=one(BO))\
                               .then_inc(att_a.sem, 1)
                        c = slot - 3
                        if 0 <= c < CHUNKS:
                            n = u * CHUNKS + c
                            act.wait_ge(f2.sem, f2.at(j, n))
                            for f in range(FC):
                                act.wait_ge(f1.sem, f1.at(j, n * FC + f + 1))
                                act.activation(h[:, f, :], bank[F1 + f % 2][:], ACT.Gelu_apprx_tanh, bias=one(BF + f))\
                                   .then_inc(hg.sem, 1)
                        c = slot - 2
                        if 0 <= c < CHUNKS:
                            n = u * CHUNKS + c
                            act.wait_ge(t_b[0].sem, t_b[0].at(j, n + 1))
                            act.wait_ge(add[1].sem, add[1].at(j, n - 2))
                            act.activation(x1[:, c % 3, :], bank[TBK][:], ACT.Identity, bias=one(B1N), scale=one(S1))\
                               .then_inc(out[0].sem, 1)
                        c = slot - 3
                        if 0 <= c < CHUNKS:
                            n = u * CHUNKS + c
                            act.wait_ge(f2.sem, f2.at(j, n + 1))
                            act.wait_ge(add[1].sem, add[1].at(j, n))
                            act.activation(ff_out[:], bank[F2][:], ACT.Gelu_apprx_tanh, bias=one(B2F))\
                               .then_inc(g2.sem, 1)
                        c = slot - 5
                        if 0 <= c < CHUNKS:
                            n = u * CHUNKS + c
                            act.wait_ge(t_b[1].sem, t_b[1].at(j, n + 1))
                            act.activation(k.state[:, c * CH:(c + 1) * CH], bank[TB2][:], ACT.Identity,
                                           bias=one(B2N), scale=one(S2)).then_inc(out[1].sem, 1)

        @block.vector
        def _(dve):
            with dve.Fori(0, LAYERS // 2) as j:
                for u in range(2):
                    dve.wait_ge(w_in[u].sem, w_in[u].at(j, 80))
                    dve.tensor_scalar(plus[u][:], col[u][:, 0:2], 1.0, None, ALU.add).then_inc(plus_in.sem, 1)
                    dve.wait_ge(plus_in.sem, plus_in.at(j, u + 1))
                    for c in range(CHUNKS + 2):
                        if c < CHUNKS:
                            n, base, r = u * CHUNKS + c, c % 2 * 3, c % 2
                            for (which, buf, m, done, clipped) in ((0, ek, kq_m, k_d, ekc), (1, eq, q_m, q_d, eqc)):
                                dve.wait_ge(m.sem, m.at(j, n + 1))
                                dve.wait_ge(done.sem, done.at(j, n - 1))
                                dve.tensor_scalar(buf[:, r, :], bank[base + (QBK if which else KB)][:],
                                                  col[u][:, BQ:BQ + 1] if which else col[u][:, BK:BK + 1], 0.0,
                                                  ALU.add, ALU.min).then_inc(clipped.sem, 1)
                        if 0 < c <= CHUNKS:
                            c -= 1
                            n, base, r = u * CHUNKS + c, c % 2 * 3, c % 2
                            dve.wait_ge(ek_a.sem, ek_a.at(j, n + 1))
                            dve.wait_ge(kv_d.sem, kv_d.at(j, n - 1))
                            dve.scalar_tensor_tensor(out=kf[:, r, :], in0=bank[base + KB][:], scalar=plus[u][:, 1:2],
                                                     in1=ek[:, r, :], op0=ALU.add, op1=ALU.max,
                                                     accum_out=sums[:, 0, c:c + 1]).then_inc(k_d.sem, 1)
                            dve.wait_ge(eq_a.sem, eq_a.at(j, n + 1))
                            dve.tensor_scalar(eq[:, r, :], eq[:, r, :], 1.0, 1.0, ALU.subtract, ALU.add)\
                               .then_inc(eqr.sem, 1)
                            dve.wait_ge(eqr.sem, eqr.at(j, n + 1))
                            dve.scalar_tensor_tensor(out=q[:, c, :], in0=bank[base + QBK][:], scalar=plus[u][:, 0:1],
                                                     in1=eq[:, r, :], op0=ALU.add, op1=ALU.max).then_inc(q_d.sem, 1)
                            dve.wait_ge(k_d.sem, k_d.at(j, n + 1))
                            dve.wait_ge(v_m.sem, v_m.at(j, n + 1))
                            dve.scalar_tensor_tensor(out=junk[:, r, :], in0=bank[base + VB][:],
                                                     scalar=col[u][:, BV:BV + 1], in1=kf[:, r, :], op0=ALU.add,
                                                     op1=ALU.mult, accum_out=sums[:, 1, c:c + 1]).then_inc(kv_d.sem, 1)
                            if c % 2:
                                b = c // 2
                                dve.wait_ge(kv_d.sem, kv_d.at(j, n + 1))
                                chain = Chain(dve, tiny, j)
                                chain.n = (u * BATCH + b) * 5
                                one = slice(b, b + 1)
                                chain.link(dve.tensor_tensor(tot[:, :, b], sums[:, :, c - 1], sums[:, :, c], ALU.add))
                                chain.link(dve.tensor_scalar(inv[:, one], tot[:, 0, one], 1e-30, None, ALU.max))
                                chain.link(dve.reciprocal(inv[:, one], inv[:, one]))
                                chain.link(dve.tensor_tensor(ratio[:, one], tot[:, 1, one], inv[:, one], ALU.mult))
                                chain.link(dve.tensor_scalar(less[:, one], ratio[:, one], -EPS_ATTN, None, ALU.mult))
                            c += 1
                        if c % 2 and c >= 3:
                            b = (c - 3) // 2
                            for cc in (2 * b, 2 * b + 1):
                                n = u * CHUNKS + cc
                                dve.wait_ge(y_a.sem, y_a.at(j, n + 1))
                                dve.tensor_scalar(q[:, cc, :], yk[:, cc % 2, :], less[:, b:b + 1], ratio[:, b:b + 1],
                                                  ALU.mult, ALU.add).then_inc(v_d.sem, 1)

                    def statistics(s, b_, c):
                        n, r = u * CHUNKS + c, c % 2
                        dve.wait_ge(t_a[s].sem, t_a[s].at(j, n + 1))
                        for t in range(TC):
                            dve.bn_stats(stats[s][:, r, t, :], b_[:, t * P:(t + 1) * P]).then_inc(st[s].sem, 1)
                        dve.wait_ge(st[s].sem, st[s].at(j, n * TC + TC))
                        dve.sem_inc(k.passed, 1)
                        for t in range(TC):
                            ins = dve.bn_aggr(mv[s][:, r, t, :], stats[s][:, r, t, :])
                        ins.then_inc(ag[s].sem, 1)

                    def normalise(s, b_, c):
                        n, r = u * CHUNKS + c, c % 2
                        dve.wait_ge(rs[s].sem, rs[s].at(j, n + 1))
                        dve.wait_ge(t_b[s].sem, t_b[s].at(j, n - 1))
                        for t in range(TC):
                            cols = slice(t * P, t * P + P)
                            ins = dve.tensor_scalar(xhat[s][:, r, cols], b_[:, cols], mv[s][:, r, t, 0:1],
                                                    rstd[s][:, r, t:t + 1], ALU.subtract, ALU.mult)
                        ins.then_inc(nm[s].sem, 1)

                    for slot in range(CHUNKS + 5):
                        if 0 <= slot - 1 < CHUNKS:
                            statistics(0, bank[TA], slot - 1)
                        if 0 <= slot - 5 < CHUNKS:
                            normalise(1, bank[TA2], slot - 5)
                        c = slot
                        if c < CHUNKS:
                            n = u * CHUNKS + c
                            dve.wait_ge(att_a.sem, att_a.at(j, n + 1))
                            dve.wait_ge(t_a[0].sem, t_a[0].at(j, n - 1))
                            dve.tensor_tensor(y[0][:, c % 2, :], att[:, c % 2, :], k.state[:, c * CH:(c + 1) * CH],
                                              ALU.add).then_inc(add[0].sem, 1)
                        if 0 <= slot - 1 < CHUNKS:
                            normalise(0, bank[TA], slot - 1)
                        c = slot - 3
                        if 0 <= c < CHUNKS:
                            n = u * CHUNKS + c
                            dve.wait_ge(g2.sem, g2.at(j, n + 1))
                            dve.wait_ge(t_a[1].sem, t_a[1].at(j, n - 1))
                            dve.tensor_tensor(y[1][:, c % 2, :], ff_out[:], x1[:, c % 3, :], ALU.add)\
                               .then_inc(add[1].sem, 1)
                        if 0 <= slot - 4 < CHUNKS:
                            statistics(1, bank[TA2], slot - 4)


def experts(nc, k, w1, w2, columns, gates_dram):
    CB1, CB2 = 0, FC
    with ExitStack() as ctx:
        w1_raw = [sbuf(ctx, nc, f"e_w1_raw{u}", [P, FF]) for u in range(2)]
        w2_raw = [sbuf(ctx, nc, f"e_w2_raw{u}", [P, FC, D]) for u in range(2)]
        w1_hi = [sbuf(ctx, nc, f"e_w1_hi{u}", [P, FF], F32R) for u in range(2)]
        w1_lo = [sbuf(ctx, nc, f"e_w1_lo{u}", [P, FF], F32R) for u in range(2)]
        w2_hi = [sbuf(ctx, nc, f"e_w2_hi{u}", [P, FC, D], F32R) for u in range(2)]
        w2_lo = [sbuf(ctx, nc, f"e_w2_lo{u}", [P, FC, D], F32R) for u in range(2)]
        col = [sbuf(ctx, nc, f"e_col{u}", [P, FC + 1]) for u in range(2)]
        gate_b = sbuf(ctx, nc, "e_gate_b", [P, 4, CH])
        h = sbuf(ctx, nc, "e_h", [P, 2, FC, CH])
        h_hi = sbuf(ctx, nc, "e_h_hi", [P, 2, FC, CH], F32R)
        h_lo = sbuf(ctx, nc, "e_h_lo", [P, 2, FC, CH], F32R)
        gated = sbuf(ctx, nc, "e_gated", [P, 2, CH])
        bank = [psum(ctx, nc, f"e_bank{i}", [P, CH]) for i in range(8)]
        N = 2 * CHUNKS

        def count(name, per=N, credit=0):
            return Count(ctx, nc, f"e_{name}", per, credit)

        w_in = [count(f"weights_in{u}", 16 * 3) for u in range(2)]
        g_in = [count(f"gates_in{i}", 16 * N // 4) for i in range(4)]
        w_hi = count("w_hi", 4)
        w_lo = count("w_lo", 4, credit=4)
        f1 = count("ff1_ready", N * FC)
        hg = count("h_gelu", N * FC, credit=4)
        hh = count("h_hi", N * FC)
        hl = count("h_lo", N * FC, credit=8)
        f2 = count("ff2_ready", N, credit=9)
        yg = count("gated", N, credit=9)
        ya = count("gate_added", N, credit=2)
        block = ctx.enter_context(nc.Block())

        @block.sync
        def _(sp):
            with sp.Fori(0, EXPERTS // 2) as j:
                for u in range(2):
                    sp.wait_ge(w_lo.sem, w_lo.at(j, 2 * u - 2))
                    sp.wait_ge(yg.sem, yg.at(j, (u - 1) * CHUNKS))
                    sp.sem_inc(k.passed, 1)
                    one = bass.ds(j * 2 + u, 1)
                    sp.dma_start(w1_raw[u][:], w1[one].rearrange("a k m -> (a k) m")).then_inc(w_in[u].sem, 16)
                    sp.dma_start(w2_raw[u][:], w2[one].rearrange("a (f k) m -> k (a f) m", k=P)).then_inc(w_in[u].sem, 16)
                    sp.dma_start(col[u][:], columns[one].rearrange("a p c -> (a p) c")).then_inc(w_in[u].sem, 16)
                    for c in range(CHUNKS):
                        n = u * CHUNKS + c
                        sp.wait_ge(yg.sem, yg.at(j, n - 3))
                        sp.sem_inc(k.passed, 1)
                        sp.dma_start(gate_b[:, c % 4, :], gates_dram[one, c * CH:(c + 1) * CH].broadcast_to([P, CH]))\
                          .then_inc(g_in[c % 4].sem, 16)

        @block.gpsimd
        def _(pool):
            for c in (w_lo, hg, hl, f2, yg, ya):
                pool.sem_inc(c.sem, c.credit)

        @block.tensor
        def _(pe):
            with pe.Fori(0, EXPERTS // 2) as j:
                for u in range(2):
                    def up(c):
                        n = u * CHUNKS + c
                        cols = slice(c * CH, c * CH + CH)
                        for f in range(FC):
                            pe.wait_ge(hg.sem, hg.at(j, n * FC + f - 3))
                            w = slice(f * P, f * P + P)
                            pe.matmul(bank[f][:], w1_hi[u][:, w], k.x_hi[:, cols], start=True, stop=False)
                            pe.matmul(bank[f][:], w1_hi[u][:, w], k.x_lo[:, cols], start=False, stop=False)
                            pe.matmul(bank[f][:], w1_lo[u][:, w], k.x_hi[:, cols], start=False, stop=True)\
                              .then_inc(f1.sem, 1)

                    def down(c):
                        n, r = u * CHUNKS + c, c % 2
                        pe.wait_ge(yg.sem, yg.at(j, n - 1))
                        for f in range(FC):
                            pe.wait_ge(hl.sem, hl.at(j, n * FC + f + 1))
                            pe.matmul(bank[4 + r][:], w2_hi[u][:, f, :], h_hi[:, r, f, :], start=(f == 0), stop=False)
                            pe.matmul(bank[4 + r][:], w2_hi[u][:, f, :], h_lo[:, r, f, :], start=False, stop=False)
                            ins = pe.matmul(bank[4 + r][:], w2_lo[u][:, f, :], h_hi[:, r, f, :], start=False,
                                            stop=(f == FC - 1))
                        ins.then_inc(f2.sem, 1)

                    pe.wait_ge(w_hi.sem, w_hi.at(j, 2 * u + 2))
                    pe.wait_ge(w_lo.sem, w_lo.at(j, 2 * u + 2))
                    for c in range(CHUNKS + 1):
                        if c < CHUNKS:
                            up(c)
                        if c:
                            down(c - 1)

        @block.scalar
        def _(act):
            with act.Fori(0, EXPERTS // 2) as j:
                for u in range(2):
                    act.wait_ge(w_in[u].sem, w_in[u].at(j, 48))
                    act.wait_ge(f2.sem, f2.at(j, (u - 1) * CHUNKS))
                    act.activation(w1_hi[u][:], w1_raw[u][:], ACT.Copy).then_inc(w_hi.sem, 1)
                    act.activation(w2_hi[u][:], w2_raw[u][:], ACT.Copy).then_inc(w_hi.sem, 1)
                    for c in range(CHUNKS):
                        n, r = u * CHUNKS + c, c % 2
                        for f in range(FC):
                            act.wait_ge(f1.sem, f1.at(j, n * FC + f + 1))
                            act.wait_ge(hl.sem, hl.at(j, n * FC + f - 7))
                            act.activation(h[:, r, f, :], bank[f][:], ACT.Gelu, bias=col[u][:, CB1 + f:CB1 + f + 1])\
                               .then_inc(hg.sem, 1)

        @block.vector
        def _(dve):
            with dve.Fori(0, EXPERTS // 2) as j:
                for u in range(2):
                    def combine(c):
                        n, r = u * CHUNKS + c, c % 2
                        dve.wait_ge(f2.sem, f2.at(j, n + 1))
                        dve.wait_ge(g_in[c % 4].sem, g_in[c % 4].at(j, 16 * (u * 2 + c // 4 + 1)))
                        dve.wait_ge(ya.sem, ya.at(j, n - 1))
                        dve.scalar_tensor_tensor(out=gated[:, r, :], in0=bank[4 + r][:],
                                                 scalar=col[u][:, CB2:CB2 + 1], in1=gate_b[:, c % 4, :],
                                                 op0=ALU.add, op1=ALU.mult).then_inc(yg.sem, 1)
                        dve.wait_ge(yg.sem, yg.at(j, n + 1))
                        s = k.state[:, c * CH:(c + 1) * CH]
                        dve.tensor_tensor(s, s, gated[:, r, :], ALU.add).then_inc(ya.sem, 1)

                    dve.wait_ge(w_hi.sem, w_hi.at(j, 2 * u + 2))
                    dve.wait_ge(f2.sem, f2.at(j, (u - 1) * CHUNKS))
                    for lo, raw, hi in ((w1_lo, w1_raw, w1_hi), (w2_lo, w2_raw, w2_hi)):
                        dve.tensor_tensor(lo[u][:], raw[u][:], hi[u][:].bitcast(F32), ALU.subtract)\
                           .then_inc(w_lo.sem, 1)
                    for c in range(CHUNKS):
                        n, r = u * CHUNKS + c, c % 2
                        dve.wait_ge(f2.sem, f2.at(j, n - 1))
                        for f in range(FC):
                            dve.wait_ge(hg.sem, hg.at(j, n * FC + f + 1))
                            dve.tensor_copy(h_hi[:, r, f, :], h[:, r, f, :]).then_inc(hh.sem, 1)
                            dve.wait_ge(hh.sem, hh.at(j, n * FC + f + 1))
                            dve.tensor_tensor(h_lo[:, r, f, :], h[:, r, f, :], h_hi[:, r, f, :].bitcast(F32),
                                              ALU.subtract).then_inc(hl.sem, 1)
                        if c:
                            combine(c - 1)
                    combine(CHUNKS - 1)


def write_out(nc, k, out):
    with ExitStack() as ctx:
        bank = [psum(ctx, nc, f"o_bank{i}", [P, CH]) for i in range(CHUNKS)]
        turned = Count(ctx, nc, "o_turned")
        added = Count(ctx, nc, "o_added")
        stored = Count(ctx, nc, "o_stored")
        block = ctx.enter_context(nc.Block())

        @block.tensor
        def _(pe):
            for c in range(CHUNKS):
                for t in range(TC):
                    at = c * CH + t * P
                    ins = pe.transpose(bank[c][:, t * P:(t + 1) * P], k.state[:, at:at + P], k.ident[:])
                ins.then_inc(turned.sem, 1)

        @block.vector
        def _(dve):
            for c in range(CHUNKS):
                dve.wait_ge(turned.sem, c + 1)
                r = flat(k.resid[:, c * TC:(c + 1) * TC, :])
                dve.tensor_tensor(r, r, bank[c][:], ALU.add).then_inc(added.sem, 1)

        @block.sync
        def _(sp):
            for c in range(CHUNKS):
                sp.wait_ge(added.sem, c + 1)
                sp.dma_start(out[c * CH:(c + 1) * CH, :].rearrange("(t p) d -> p t d", p=P),
                             k.resid[:, c * TC:(c + 1) * TC, :]).then_inc(stored.sem, 16)
            sp.wait_ge(stored.sem, 16 * CHUNKS)


class Kept:
    pass


def program(nc, x, wqkv, bqk, bv, wo, wo_bias, ghost, w_gate, w_up, w_down,
            l_wqkv, l_wo, l_w1, l_w2, l_columns, router_w, router_b, e_w1, e_w2, e_columns, out):
    with ExitStack() as ctx:
        k = Kept()
        k.passed = ctx.enter_context(nc.semaphore("waits_passed"))
        k.ident = sbuf(ctx, nc, "ident", [P, P])
        k.identb = sbuf(ctx, nc, "identb", [P, P], BF16)
        k.maskb = sbuf(ctx, nc, "maskb", [P, P], BF16)
        k.eps_outer = sbuf(ctx, nc, "eps_outer", [P, 1])
        k.eps_ln = sbuf(ctx, nc, "eps_ln", [P, 1])
        k.resid = sbuf(ctx, nc, "resid", [P, TILES, D])
        k.mv = sbuf(ctx, nc, "mean_var", [P, TILES, 2])
        k.rstd = sbuf(ctx, nc, "rstd", [P, TILES])
        k.x_hi = sbuf(ctx, nc, "x_hi", [P, BATCH * SEQ], F32R)
        k.x_lo = sbuf(ctx, nc, "x_lo", [P, BATCH * SEQ], F32R)
        gates_dram = nc.dram_tensor("gates_dram", [EXPERTS, BATCH * SEQ], F32, kind="Internal").ap()

        build_constants(nc, k)
        load(nc, k, x)
        outer_statistics(nc, k, "n1")
        quantized_feed_forward(nc, k, w_gate, w_up, w_down, wo_bias)
        attention(nc, k, wqkv, bqk, bv, wo, ghost)
        outer_statistics(nc, k, "n2")
        k.state = sbuf(ctx, nc, "state", [P, BATCH * SEQ])
        second_norm_and_routing(nc, k, router_w, router_b, gates_dram)
        linear_layers(nc, k, l_wqkv, l_wo, l_w1, l_w2, l_columns)
        experts(nc, k, e_w1, e_w2, e_columns, gates_dram)
        write_out(nc, k, out)


def load(nc, k, x):
    with ExitStack() as ctx:
        loaded = Count(ctx, nc, "x_loaded")
        block = ctx.enter_context(nc.Block())

        @block.sync
        def _(sp):
            for b in range(BATCH):
                sp.dma_start(k.resid[:, b * TB:(b + 1) * TB, :],
                             x[b * SEQ:(b + 1) * SEQ, :].rearrange("(t p) d -> p t d", p=P)).then_inc(loaded.sem, 16)
            sp.wait_ge(loaded.sem, 16 * BATCH)


def kernel(**inputs):
    import numpy as np
    import concourse.bacc as bacc
    from concourse.bass_utils import run_bass_kernel_spmd

    a = {n: np.asarray(v) for n, v in inputs.items()}
    wt = a["L0_attn_Wqkv_w"].T.reshape(D, 3, PAIRS, 2, DH)
    qk = np.repeat(wt[:, :2].transpose(2, 0, 1, 3, 4)[:, :, :, :, None, :], 2, axis=4).reshape(PAIRS, D, 4 * P)
    v = wt[:, 2].transpose(1, 0, 2, 3).reshape(PAIRS, D, P)
    bt = a["L0_attn_Wqkv_b"].reshape(3, PAIRS, 2, DH)
    bqk = np.repeat(bt[:2].transpose(1, 0, 2, 3)[:, :, :, None, :], 2, axis=3).reshape(PAIRS, 4, P)
    l = {n[8:]: v_ for n, v_ in a.items() if n.startswith("L1_attn_")}
    l_columns = np.stack([l["bq"], l["bk"], l["bv"], l["bo"], l["ln1_s"], l["ln1_b"],
                          *l["b1"].reshape(LAYERS, FC, P).transpose(1, 0, 2), l["b2"], l["ln2_s"], l["ln2_b"]],
                         axis=-1)
    e_columns = np.stack([*a["L1_ffn_b1"].reshape(EXPERTS, FC, P).transpose(1, 0, 2), a["L1_ffn_b2"]], axis=-1)
    arrays = {
        "x": a["L0_attn_inputs"].reshape(BATCH * SEQ, D), "wqkv": np.concatenate([qk, v], axis=2),
        "bqk": bqk.transpose(0, 2, 1), "bv": bt[2].reshape(-1), "wo": a["L0_attn_Wo_w"].T,
        "wo_bias": a["L0_attn_Wo_b"], "ghost": a["L0_attn_ghost"],
        "w_gate": a["L0_ffn_w_gate"], "w_up": a["L0_ffn_w_up"], "w_down": a["L0_ffn_w_down"],
        "l_wqkv": np.stack([l["Wq"], l["Wk"], l["Wv"]], axis=1), "l_wo": l["Wo"], "l_w1": l["W1"], "l_w2": l["W2"],
        "l_columns": l_columns, "router_w": a["L1_ffn_router_w"], "router_b": a["L1_ffn_router_b"],
        "e_w1": a["L1_ffn_w1"], "e_w2": a["L1_ffn_w2"], "e_columns": e_columns,
    }
    arrays = {n: np.ascontiguousarray(v_) for n, v_ in arrays.items()}
    nc = bacc.Bacc("TRN2", target_bir_lowering=False, num_devices=1)
    args = {n: nc.dram_tensor(f"in_{n}", v_.shape, mybir.dt.from_np(v_.dtype), kind="ExternalInput").ap()
            for n, v_ in arrays.items()}
    out = nc.dram_tensor("out", [BATCH * SEQ, D], F32, kind="ExternalOutput").ap()
    program(nc, out=out, **args)
    r = run_bass_kernel_spmd(nc, [{f"in_{n}": v_ for n, v_ in arrays.items()}], core_ids=[0])
    return r.results[0]["out"].reshape(BATCH, SEQ, D)
```

```python
from contextlib import ExitStack

import concourse.bass as bass
from concourse import mybir

ALU = mybir.AluOpType
ACT = mybir.ActivationFunctionType
AX = mybir.AxisListType
F32 = mybir.dt.float32
F32R = mybir.dt.float32r
BF16 = mybir.dt.bfloat16
U32 = mybir.dt.uint32

P = 128
BATCH, SEQ, D = 4, 1024, 128
TILES = BATCH * SEQ // P
TB = SEQ // P
CH = 512
CHUNKS = BATCH * SEQ // CH
TC = CH // P
HEADS, DH = 16, 64
PAIRS = HEADS // 2
INNER = 352
IC = [(0, 128), (128, 128), (256, 96)]
QB = 16
LAYERS, FF, FC = 8, 512, 4
EXPERTS = 8
EPS_OUTER, EPS_LN, EPS_ATTN = 1e-5, 1e-6, 1e-6
MASKED = -1e30


class Count:

    def __init__(self, ctx, nc, name, per_turn=0, credit=0):
        self.sem = ctx.enter_context(nc.semaphore(name))
        self.per_turn, self.credit = per_turn, credit

    def at(self, turn, n):
        return turn * self.per_turn + (n + self.credit)


def sbuf(ctx, nc, name, shape, dt=F32):
    return ctx.enter_context(nc.sbuf_tensor(name, shape, dt))


def psum(ctx, nc, name, shape, dt=F32):
    return ctx.enter_context(nc.psum_tensor(name, shape, dt))


class Chain:

    def __init__(self, eng, count, turn=0):
        self.eng, self.count, self.turn, self.n = eng, count, turn, 0

    def link(self, ins):
        self.n += 1
        ins.then_inc(self.count.sem, 1)
        self.eng.wait_ge(self.count.sem, self.count.at(self.turn, self.n))


HALVES, ONES, TWOS = 1.5 * 2 ** 22, 1.5 * 2 ** 23, 1.5 * 2 ** 24
BELOW = 1.0 - 2.0 ** -24


def fp4_round_trip(dve, chain, src, dst, bmax, scale, rinv, t0, t1, t2, t3, nb):
    def blocks(t):
        return t.rearrange("p (n q) -> p n q", q=QB)

    def spread(t):
        return t.unsqueeze(2).broadcast_to([t.shape[0], nb, QB])

    link = chain.link
    link(dve.tensor_reduce(bmax, blocks(src), AX.X, ALU.max, apply_absolute_value=True))
    link(dve.tensor_scalar(scale, bmax, 1.0 / 6.0, 1e-12, ALU.mult, ALU.max))
    link(dve.reciprocal(rinv, scale))
    link(dve.tensor_scalar(rinv, rinv, BELOW, None, ALU.mult))
    link(dve.tensor_tensor(blocks(t0), blocks(src), spread(rinv), ALU.mult))
    link(dve.tensor_scalar(t0.bitcast(U32), t0.bitcast(U32), 0x7FFFFFFF, None, ALU.bitwise_and))
    link(dve.tensor_scalar(t1, t0, 2.0, HALVES, ALU.min, ALU.add))
    link(dve.tensor_scalar(t2, t0, 2.0, ONES, ALU.max, ALU.add))
    link(dve.tensor_scalar(t3, t0, 4.0, TWOS, ALU.max, ALU.add))
    link(dve.tensor_scalar(t2, t2, ONES + 4.0, ONES, ALU.min, ALU.subtract))
    link(dve.scalar_tensor_tensor(out=t1, in0=t1, scalar=HALVES, in1=t2, op0=ALU.subtract, op1=ALU.add))
    link(dve.scalar_tensor_tensor(out=t0, in0=t3, scalar=TWOS + 6.0, in1=t1, op0=ALU.subtract, op1=ALU.add))
    link(dve.scalar_tensor_tensor(out=t2.bitcast(U32), in0=src.bitcast(U32), scalar=0x80000000,
                                  in1=t0.bitcast(U32), op0=ALU.bitwise_and, op1=ALU.bitwise_or))
    link(dve.tensor_tensor(blocks(dst), blocks(t2), spread(scale), ALU.mult))


FP4_LINKS = 14


def inverse_root(dve, chain, out, var, root, eps, half, t0):
    link = chain.link
    link(dve.reciprocal(out, root))
    link(dve.tensor_scalar(half, var, eps, -0.5, ALU.add, ALU.mult))
    link(dve.tensor_tensor(t0, out, out, ALU.mult))
    link(dve.tensor_tensor(t0, t0, half, ALU.mult))
    link(dve.scalar_tensor_tensor(out=out, in0=t0, scalar=1.5, in1=out, op0=ALU.add, op1=ALU.mult))


ROOT_LINKS = 5


def build_constants(nc, k):
    with ExitStack() as ctx:
        made = Count(ctx, nc, "constants_made")
        block = ctx.enter_context(nc.Block())

        @block.gpsimd
        def _(pool):
            pool.memset(k.ident[:], 0.0).then_inc(made.sem, 1)
            pool.memset(k.maskb[:], 0.0).then_inc(made.sem, 1)
            pool.memset(k.eps_outer[:], EPS_OUTER).then_inc(made.sem, 1)
            pool.memset(k.eps_ln[:], EPS_LN).then_inc(made.sem, 1)
            pool.memset(k.identb[:], 0.0).then_inc(made.sem, 1)
            pool.wait_ge(made.sem, 5)
            for t in (k.ident, k.identb):
                pool.affine_select(out=t[:], in_=t[:], compare_op=ALU.not_equal, fill=1.0, base=0,
                                   pattern=[[-1, P]], channel_multiplier=1)
            pool.affine_select(out=k.maskb[:], in_=k.maskb[:], compare_op=ALU.is_ge, fill=MASKED, base=0,
                               pattern=[[-1, P]], channel_multiplier=1)


def outer_statistics(nc, k, name):
    with ExitStack() as ctx:
        stats = sbuf(ctx, nc, f"{name}_stats", [P, TILES, 6])
        root = sbuf(ctx, nc, f"{name}_root", [P, TILES])
        half = sbuf(ctx, nc, f"{name}_half", [P, TILES])
        t0 = sbuf(ctx, nc, f"{name}_t0", [P, TILES])
        stat = Count(ctx, nc, f"{name}_stat")
        aggregated = Count(ctx, nc, f"{name}_aggregated")
        rooted = Count(ctx, nc, f"{name}_rooted")
        steps = Count(ctx, nc, f"{name}_steps")
        block = ctx.enter_context(nc.Block())

        @block.vector
        def _(dve):
            with dve.Fori(0, TILES // TC) as c:
                for t in range(TC):
                    dve.bn_stats(stats[:, bass.ds(c * TC + t, 1), :], k.resid[:, bass.ds(c * TC + t, 1), :])\
                       .then_inc(stat.sem, 1)
            dve.wait_ge(stat.sem, TILES)
            for t in range(TILES):
                ins = dve.bn_aggr(k.mv[:, t, :], stats[:, t, :])
            ins.then_inc(aggregated.sem, 1)
            dve.wait_ge(rooted.sem, 1)
            inverse_root(dve, Chain(dve, steps), k.rstd[:], k.mv[:, :, 1], root[:], EPS_OUTER, half[:], t0[:])

        @block.scalar
        def _(act):
            act.wait_ge(aggregated.sem, 1)
            act.activation(root[:], k.mv[:, :, 1], ACT.Sqrt, bias=k.eps_outer[:]).then_inc(rooted.sem, 1)


def normalise_chunk(dve, k, c, xn, done):
    for t in range(TC):
        i = c * TC + t
        dve.tensor_scalar(xn[:, t, :], k.resid[:, bass.ds(i, 1), :].rearrange("p a d -> p (a d)"),
                          k.mv[:, bass.ds(i, 1), 0], k.rstd[:, bass.ds(i, 1)],
                          ALU.subtract, ALU.mult).then_inc(done.sem, 1)


def flat(t):
    return t.rearrange("p t d -> p (t d)")


def quantized_feed_forward(nc, k, w_gate, w_up, w_down, wo_bias):
    GU = 2 * INNER
    with ExitStack() as ctx:
        w_rows = sbuf(ctx, nc, "w_rows", [P, 6, D])
        wq_rows = sbuf(ctx, nc, "wq_rows", [P, 6, D])
        wd_rows = sbuf(ctx, nc, "wd_rows", [P, INNER])
        wdq_rows = sbuf(ctx, nc, "wdq_rows", [P, INNER])
        bias_b = sbuf(ctx, nc, "bias_b", [P, D])
        wguT = sbuf(ctx, nc, "wguT", [P, GU])
        wdT = sbuf(ctx, nc, "wdT", [P, 3, D])
        HN = TC * INNER
        tmp = [sbuf(ctx, nc, f"fp4_tmp{i}", [P, HN]) for i in range(4)]
        small = [sbuf(ctx, nc, f"fp4_small{i}", [P, HN // QB]) for i in range(3)]
        xn = sbuf(ctx, nc, "xn", [P, TC, D])
        xq = sbuf(ctx, nc, "xq", [P, CH])
        xqT = sbuf(ctx, nc, "xqT", [P, CH])
        silu = sbuf(ctx, nc, "silu_gate", [P, 2, INNER])
        h = sbuf(ctx, nc, "h", [P, TC, INNER])
        hq = sbuf(ctx, nc, "hq", [P, TC, INNER])
        hqT = sbuf(ctx, nc, "hqT", [P, 2, 3, D])
        bank = [psum(ctx, nc, f"ffn_bank{i}", [P, CH]) for i in range(8)]

        def scratch(n):
            return [t[:, 0:n // QB] for t in small] + [t[:, 0:n] for t in tmp]

        loaded = Count(ctx, nc, "ffn_loaded")
        cleared = Count(ctx, nc, "ffn_cleared")
        wlinks = Count(ctx, nc, "ffn_weight_links")
        wturned = Count(ctx, nc, "ffn_weight_turned")
        wkept = Count(ctx, nc, "ffn_weight_kept")
        with nc.Block() as block:
            @block.sync
            def _(sp):
                for i, w in enumerate((w_gate, w_up)):
                    sp.dma_start(w_rows[:, 3 * i:3 * i + 2, :],
                                 w[0:2 * P, :].rearrange("(t p) d -> p t d", p=P)).then_inc(loaded.sem, 16)
                    sp.dma_start(w_rows[0:96, 3 * i + 2, :], w[2 * P:INNER, :]).then_inc(loaded.sem, 16)
                sp.dma_start(wd_rows[:], w_down).then_inc(loaded.sem, 16)
                sp.dma_start(bias_b[:], wo_bias.rearrange("(a d) -> a d", a=1).broadcast_to([P, D]))\
                  .then_inc(loaded.sem, 16)

            @block.vector
            def _(dve):
                dve.memset(w_rows[96:P, 2, :], 0.0).then_inc(cleared.sem, 1)
                dve.memset(w_rows[96:P, 5, :], 0.0).then_inc(cleared.sem, 1)
                dve.wait_ge(cleared.sem, 2)
                dve.wait_ge(loaded.sem, 96)
                chain = Chain(dve, wlinks)
                n = 6 * D
                fp4_round_trip(dve, chain, w_rows[:].rearrange("p t d -> p (t d)"),
                               wq_rows[:].rearrange("p t d -> p (t d)"), *scratch(n), n // QB)
                fp4_round_trip(dve, chain, wd_rows[:], wdq_rows[:], *scratch(INNER), INNER // QB)

            @block.tensor
            def _(pe):
                pe.wait_ge(wlinks.sem, FP4_LINKS)
                for j in range(6):
                    pe.transpose(bank[j // 3][:, j % 3 * P:(j % 3 + 1) * P], wq_rows[:, j, :], k.ident[:])\
                      .then_inc(wturned.sem, 1)
                pe.wait_ge(wlinks.sem, 2 * FP4_LINKS)
                for j, (at, w) in enumerate(IC):
                    pe.transpose(bank[2][0:w, j * P:(j + 1) * P], wdq_rows[:, at:at + w], k.ident[:])\
                      .then_inc(wturned.sem, 1)

            @block.scalar
            def _(act):
                for i in range(2):
                    act.wait_ge(wturned.sem, 3 * i + 3)
                    act.activation(wguT[:, i * INNER:(i + 1) * INNER], bank[i][:, 0:INNER], ACT.Copy)
                act.wait_ge(wturned.sem, 9)
                for j, (at, w) in enumerate(IC):
                    act.activation(wdT[0:w, j, :], bank[2][0:w, j * P:(j + 1) * P], ACT.Copy)


        normed = Count(ctx, nc, "x_normed", TC)
        turned = Count(ctx, nc, "x_turned", 1)
        hi_kept = Count(ctx, nc, "x_hi_kept", 1, credit=1)
        lo_kept = Count(ctx, nc, "x_lo_kept", 1, credit=1)
        links = Count(ctx, nc, "ffn_links", 2 * FP4_LINKS)
        xq_turned = Count(ctx, nc, "xq_turned", 1)
        xq_kept = Count(ctx, nc, "xq_kept", 1, credit=1)
        gated = Count(ctx, nc, "gate_up_ready", TC)
        silu_done = Count(ctx, nc, "silu_ready", TC)
        h_done = Count(ctx, nc, "h_ready", TC, credit=2)
        hq_turned = Count(ctx, nc, "hq_turned", TC)
        hq_kept = Count(ctx, nc, "hq_kept", TC, credit=1)
        downed = Count(ctx, nc, "down_ready", TC)
        added = Count(ctx, nc, "ffn_added", 1, credit=1)
        GATE, UP, HT, DOWN = 2, 4, 6, 7
        def down(pe, c, t):
            for j, (at, w) in enumerate(IC):
                ins = pe.matmul(bank[DOWN][:, t * P:(t + 1) * P], hqT[0:w, t % 2, j, :], wdT[0:w, j, :],
                                start=(j == 0), stop=(j == 2))
            ins.then_inc(downed.sem, 1)

        with nc.Block() as block:
            @block.tensor
            def _(pe):
                with pe.Fori(0, CHUNKS) as c:
                    pe.wait_ge(normed.sem, normed.at(c, TC))
                    pe.wait_ge(hi_kept.sem, hi_kept.at(c, 0))
                    pe.wait_ge(lo_kept.sem, lo_kept.at(c, 0))
                    for t in range(TC):
                        ins = pe.transpose(bank[0][:, t * P:(t + 1) * P], xn[:, t, :], k.ident[:])
                    ins.then_inc(turned.sem, 1)
                    pe.wait_ge(links.sem, links.at(c, FP4_LINKS))
                    pe.wait_ge(xq_kept.sem, xq_kept.at(c, 0))
                    for t in range(TC):
                        ins = pe.transpose(bank[1][:, t * P:(t + 1) * P], xq[:, t * P:(t + 1) * P], k.ident[:])
                    ins.then_inc(xq_turned.sem, 1)
                    pe.wait_ge(xq_kept.sem, xq_kept.at(c, 1))
                    for t in range(TC):
                        pe.wait_ge(h_done.sem, h_done.at(c, t - 1))
                        for b, at in ((GATE, 0), (UP, INNER)):
                            ins = pe.matmul(bank[b + t % 2][:, 0:INNER], xqT[:, t * P:(t + 1) * P],
                                            wguT[:, at:at + INNER], start=True, stop=True)
                        ins.then_inc(gated.sem, 1)
                    pe.wait_ge(links.sem, links.at(c, 2 * FP4_LINKS))
                    pe.wait_ge(added.sem, added.at(c, 0))
                    for t in range(TC):
                        pe.wait_ge(hq_kept.sem, hq_kept.at(c, t))
                        for j, (at, w) in enumerate(IC):
                            ins = pe.transpose(bank[HT][0:w, j * P:(j + 1) * P], hq[:, t, at:at + w], k.ident[:])
                        ins.then_inc(hq_turned.sem, 1)
                        if t:
                            down(pe, c, t - 1)
                    pe.wait_ge(hq_kept.sem, hq_kept.at(c, TC))
                    down(pe, c, TC - 1)

            @block.scalar
            def _(act):
                with act.Fori(0, CHUNKS) as c:
                    act.wait_ge(turned.sem, turned.at(c, 1))
                    act.sem_inc(k.passed, 1)
                    act.activation(k.x_hi[:, bass.ds(c * CH, CH)], bank[0][:], ACT.Copy).then_inc(hi_kept.sem, 1)
                    act.wait_ge(xq_turned.sem, xq_turned.at(c, 1))
                    act.activation(xqT[:], bank[1][:], ACT.Copy).then_inc(xq_kept.sem, 1)
                    for t in range(TC):
                        act.wait_ge(gated.sem, gated.at(c, t + 1))
                        act.activation(silu[:, t % 2, :], bank[GATE + t % 2][:, 0:INNER], ACT.Silu)\
                           .then_inc(silu_done.sem, 1)
                    for t in range(TC):
                        act.wait_ge(hq_turned.sem, hq_turned.at(c, t + 1))
                        if t >= 2:
                            act.wait_ge(downed.sem, downed.at(c, t - 1))
                        act.activation(hqT[:, t % 2, 0:2, :].rearrange("p a d -> p (a d)"),
                                       bank[HT][:, 0:2 * P], ACT.Copy)
                        act.activation(hqT[0:96, t % 2, 2, :], bank[HT][0:96, 2 * P:3 * P], ACT.Copy)\
                           .then_inc(hq_kept.sem, 1)

            @block.vector
            def _(dve):
                with dve.Fori(0, CHUNKS) as c:
                    normalise_chunk(dve, k, c, xn, normed)
                    dve.wait_ge(normed.sem, normed.at(c, TC))
                    chain = Chain(dve, links, c)
                    fp4_round_trip(dve, chain, flat(xn[:]), xq[:], *scratch(CH), CH // QB)
                    dve.wait_ge(hi_kept.sem, hi_kept.at(c, 1))
                    dve.tensor_tensor(k.x_lo[:, bass.ds(c * CH, CH)], bank[0][:],
                                      k.x_hi[:, bass.ds(c * CH, CH)].bitcast(F32), ALU.subtract).then_inc(lo_kept.sem, 1)
                    for t in range(TC):
                        dve.wait_ge(silu_done.sem, silu_done.at(c, t + 1))
                        dve.tensor_tensor(h[:, t, :], bank[UP + t % 2][:, 0:INNER], silu[:, t % 2, :],
                                          ALU.mult).then_inc(h_done.sem, 1)
                    dve.wait_ge(h_done.sem, h_done.at(c, TC))
                    fp4_round_trip(dve, chain, flat(h[:]), flat(hq[:]), *scratch(HN), HN // QB)
                    dve.wait_ge(downed.sem, downed.at(c, TC))
                    out = k.resid[:, bass.ds(c * TC, TC), :]
                    dve.tensor_tensor(flat(out), flat(out), bank[DOWN][:], ALU.add).then_inc(added.sem, 1)
                dve.wait_ge(added.sem, added.at(CHUNKS, 0))
                dve.tensor_tensor(k.resid[:], k.resid[:],
                                  bias_b[:].unsqueeze(1).broadcast_to([P, TILES, D]), ALU.add)

            @block.gpsimd
            def _(pool):
                for count in (hi_kept, lo_kept, xq_kept, h_done, hq_kept, added):
                    pool.sem_inc(count.sem, count.credit)


def attention(nc, k, wqkv, bqk, bv, wo, ghost):
    QK = 4 * P
    with ExitStack() as ctx:
        w_raw = sbuf(ctx, nc, "w_raw", [P, PAIRS + 1, QK + P])
        w_hi = sbuf(ctx, nc, "w_hi", [P, QK + P], F32R)
        w_lo = sbuf(ctx, nc, "w_lo", [P, QK + P], F32R)
        bqk_sb = sbuf(ctx, nc, "bqk_sb", [P, PAIRS + 1, 4])
        bias_now = sbuf(ctx, nc, "bias_now", [P, 4])
        bv_b = sbuf(ctx, nc, "bv_b", [P, PAIRS, P])
        wo_sb = sbuf(ctx, nc, "wo_sb", [P, PAIRS, D])
        ghost_b = sbuf(ctx, nc, "ghost_b", [P, PAIRS, 2])
        xb_hi = sbuf(ctx, nc, "xb_hi", [P, SEQ], F32R)
        xb_lo = sbuf(ctx, nc, "xb_lo", [P, SEQ], F32R)
        q_s = sbuf(ctx, nc, "q_stacked", [P, 2, SEQ], F32R)
        k_hi = sbuf(ctx, nc, "k_high", [P, 2, SEQ], F32R)
        k_lo = sbuf(ctx, nc, "k_low", [P, 2, SEQ], F32R)
        v_sb = sbuf(ctx, nc, "v_sb", [P, TB, P])
        prob = sbuf(ctx, nc, "prob", [P, 2, SEQ])
        probT = [[sbuf(ctx, nc, f"probT{h}{g}", [P, 4 * (g + 1), CH]) for g in range(2)] for h in range(2)]
        negmax = sbuf(ctx, nc, "negmax", [P, 2, TB])
        den = sbuf(ctx, nc, "den", [P, 2, TB])
        rden = sbuf(ctx, nc, "rden", [P, 2, TB])
        av_raw = sbuf(ctx, nc, "av_raw", [P, CH])
        av_sb = sbuf(ctx, nc, "av_sb", [P, CH])
        score = psum(ctx, nc, "score", [P, 2, SEQ])
        turn_bank = psum(ctx, nc, "turn_bank", [P, 2, CH])
        av = psum(ctx, nc, "av", [P, CH])
        rb = psum(ctx, nc, "rb", [P, CH])
        fresh = score[:].rearrange("p a (b n) -> p (a b) n", n=CH)

        loaded = Count(ctx, nc, "attn_loaded")
        scaled = Count(ctx, nc, "bq_scaled")
        bias_in = Count(ctx, nc, "bias_in", 1)
        xb_kept = Count(ctx, nc, "xb_kept", 2)
        w_split = Count(ctx, nc, "w_hi_split", 2)
        w_rest = Count(ctx, nc, "w_lo_split", 2)
        proj = Count(ctx, nc, "qk_projected", 8, credit=1)
        hi_out = Count(ctx, nc, "qk_hi_out", 8)
        lo_out = Count(ctx, nc, "qk_lo_out", 8, credit=4)
        v_proj = Count(ctx, nc, "v_projected", 2, credit=2)
        v_out = Count(ctx, nc, "v_out", 2)
        scored = Count(ctx, nc, "scored", 2 * TB)
        maxed = Count(ctx, nc, "maxed", 2 * TB)
        exped = Count(ctx, nc, "exped", 2 * TB, credit=1)
        turned = Count(ctx, nc, "prob_turned", 24, credit=1)
        kept_act = Count(ctx, nc, "probT_kept_by_act", 12, credit=1)
        kept_dve = Count(ctx, nc, "probT_kept_by_dve", 12, credit=1)
        summed = Count(ctx, nc, "av_ready", 2)
        r_links = Count(ctx, nc, "rden_links", 4)
        spread = Count(ctx, nc, "rden_spread", 2)
        av_out = Count(ctx, nc, "av_out", 2)
        av_done = Count(ctx, nc, "av_normalised", 2, credit=1)
        outed = Count(ctx, nc, "wo_ready", 2, credit=1)
        added = Count(ctx, nc, "attn_added", 2, credit=1)

        def chunks(i):
            return [(b, min(b + TC, i + 1)) for b in range(0, i + 1, TC)]

        order, e = {}, 0
        for i in range(TB):
            for hd in range(2):
                for c in range(len(chunks(i))):
                    order[i, hd, c] = e
                    e += 1
        assert e == 24
        group_end = [order[3, 1, 0] + 1, 24]

        def keep_turned(eng, mine, count, turn, i, hd, copy):
            for c, (b0, b1) in enumerate(chunks(i)):
                e = order[i, hd, c]
                if e % 2 != mine:
                    continue
                eng.wait_ge(turned.sem, turned.at(turn, e + 1))
                n = b1 - b0
                at = i % TC * P
                copy(probT[hd][i // TC][:, b0:b1, at:at + P],
                     turn_bank[:, e % 2, 0:n * P].rearrange("p (b n) -> p b n", n=P)).then_inc(count.sem, 1)

        block = ctx.enter_context(nc.Block())

        @block.sync
        def _(sp):
            for to, of in ((slice(0, PAIRS), slice(0, PAIRS)), (slice(PAIRS, PAIRS + 1), slice(0, 1))):
                sp.dma_start(w_raw[:, to, :], wqkv[of].rearrange("a k m -> k a m")).then_inc(loaded.sem, 16)
                sp.dma_start(bqk_sb[:, to, :], bqk[of].rearrange("a p m -> p a m")).then_inc(loaded.sem, 16)
            sp.dma_start(bv_b[:].rearrange("p a m -> p (a m)"),
                         bv.rearrange("(a n) -> a n", a=1).broadcast_to([P, HEADS * DH])).then_inc(loaded.sem, 16)
            sp.dma_start(wo_sb[:], wo.rearrange("(a p) m -> p a m", p=P)).then_inc(loaded.sem, 16)
            sp.dma_start(ghost_b[:].rearrange("p a m -> p (a m)"),
                         ghost.rearrange("(a n) -> a n", a=1).broadcast_to([P, HEADS])).then_inc(loaded.sem, 16)

        @block.gpsimd
        def _(pool):
            for count in (proj, lo_out, v_proj, exped, turned, kept_act, kept_dve, av_done, outed, added):
                pool.sem_inc(count.sem, count.credit)

        @block.tensor
        def _(pe):
            def project_qk(turn):
                pe.wait_ge(w_split.sem, w_split.at(turn, 2))
                pe.wait_ge(w_rest.sem, w_rest.at(turn, 2))
                pe.wait_ge(exped.sem, exped.at(turn, 0))
                for n in range(8):
                    pe.wait_ge(lo_out.sem, lo_out.at(turn, n - 3))
                    w = slice(n // 2 * P, n // 2 * P + P)
                    x = slice(n % 2 * CH, n % 2 * CH + CH)
                    pe.matmul(fresh[:, n % 4, :], w_hi[:, w], xb_hi[:, x], start=True, stop=False)
                    pe.matmul(fresh[:, n % 4, :], w_hi[:, w], xb_lo[:, x], start=False, stop=False)
                    pe.matmul(fresh[:, n % 4, :], w_lo[:, w], xb_hi[:, x], start=False, stop=True)\
                      .then_inc(proj.sem, 1)

            def project_v(turn, u):
                if u:
                    pe.wait_ge(v_out.sem, v_out.at(turn, 1))
                else:
                    pe.wait_ge(av_done.sem, av_done.at(turn, 0))
                for t in range(TC):
                    to = rb[:, t * P:t * P + P]
                    x = slice((u * TC + t) * P, (u * TC + t) * P + P)
                    pe.matmul(to, xb_hi[:, x], w_hi[:, QK:], start=True, stop=False)
                    pe.matmul(to, xb_hi[:, x], w_lo[:, QK:], start=False, stop=False)
                    ins = pe.matmul(to, xb_lo[:, x], w_hi[:, QK:], start=False, stop=True)
                ins.then_inc(v_proj.sem, 1)

            def scores(i, hd):
                q = q_s[:, hd, i * P:i * P + P]
                width = (i + 1) * P
                for c0 in range(0, width, CH):
                    c1 = min(c0 + CH, width)
                    pe.matmul(score[:, hd, c0:c1], q, k_hi[:, hd, c0:c1], start=True, stop=False)
                    pe.matmul(score[:, hd, c0:c1], q, k_lo[:, hd, c0:c1], start=False, stop=(c1 < width))
                pe.matmul(score[:, hd, i * P:width], k.identb[:], k.maskb[:], start=False, stop=True)\
                  .then_inc(scored.sem, 1)

            def turns(turn, i, hd):
                for c, (b0, b1) in enumerate(chunks(i)):
                    e = order[i, hd, c]
                    count = kept_dve if e % 2 else kept_act
                    pe.wait_ge(count.sem, count.at(turn, e // 2))
                    for blk in range(b0, b1):
                        ins = pe.transpose(turn_bank[:, e % 2, (blk - b0) * P:(blk - b0 + 1) * P],
                                           prob[:, hd, blk * P:(blk + 1) * P], k.ident[:])
                    ins.then_inc(turned.sem, 1)

            def values(turn, g, b0, b1):
                nb = TC * (g + 1)
                if b0 == 0:
                    pe.wait_ge(kept_act.sem, kept_act.at(turn, group_end[g] // 2))
                    pe.wait_ge(kept_dve.sem, kept_dve.at(turn, group_end[g] // 2))
                    pe.wait_ge(added.sem, added.at(turn, g))
                for blk in range(b0, b1):
                    c0 = max(blk - TC * g, 0) * P
                    for hd in range(2):
                        r = slice(hd * DH, hd * DH + DH)
                        ins = pe.matmul(av[r, c0:CH], v_sb[:, blk, r], probT[hd][g][:, blk, c0:CH],
                                        start=(blk == 0), stop=(blk == nb - 1))
                if b1 == nb:
                    ins.then_inc(summed.sem, 1)

            def spread_rden(turn, g):
                pe.wait_ge(r_links.sem, r_links.at(turn, 2 * g + 2))
                for t in range(TC):
                    for hd in range(2):
                        i = g * TC + t
                        ins = pe.matmul(rb[hd * DH:(hd + 1) * DH, t * P:(t + 1) * P],
                                        rden[:, hd, i:i + 1].broadcast_to([P, DH]), k.ident[:],
                                        start=True, stop=True)
                ins.then_inc(spread.sem, 1)

            def output(turn, p, g):
                pe.wait_ge(av_done.sem, av_done.at(turn, g + 1))
                for t in range(TC):
                    ins = pe.matmul(av[:, t * P:(t + 1) * P], av_sb[:, t * P:(t + 1) * P],
                                    wo_sb[:, bass.ds(p, 1), :].rearrange("p a d -> p (a d)"),
                                    start=True, stop=True)
                ins.then_inc(outed.sem, 1)

            def body(turn, p, last):
                project_qk(turn)
                if last:
                    values(turn - 1, 1, 0, 2)
                pe.wait_ge(lo_out.sem, lo_out.at(turn, 8))
                scores(0, 0)
                scores(0, 1)
                if last:
                    values(turn - 1, 1, 2, 4)
                for i in range(TB):
                    for hd in range(2):
                        pe.wait_ge(exped.sem, exped.at(turn, 2 * i + hd + 1))
                        turns(turn, i, hd)
                        if i + 1 < TB:
                            scores(i + 1, hd)
                        if last and i < 2:
                            values(turn - 1, 1, 4 + 2 * i + hd, 5 + 2 * i + hd)
                        if (i, hd) == (1, 1) and last:
                            spread_rden(turn - 1, 1)
                        if (i, hd) == (3, 0):
                            if last:
                                output(turn - 1, p - 1, 1)
                            project_v(turn, 0)
                        if (i, hd) == (4, 0):
                            project_v(turn, 1)
                        if (i, hd) == (5, 0):
                            pe.wait_ge(v_out.sem, v_out.at(turn, 2))
                            values(turn, 0, 0, 2)
                        if (i, hd) == (5, 1):
                            values(turn, 0, 2, 4)
                            spread_rden(turn, 0)
                        if (i, hd) == (7, 0):
                            output(turn, p, 0)

            with pe.Fori(0, BATCH) as b:
                pe.wait_ge(xb_kept.sem, xb_kept.at(b, 2))
                body(b * PAIRS, 0, False)
                with pe.Fori(1, PAIRS) as p:
                    body(b * PAIRS + p, p, True)
                turn = b * PAIRS + (PAIRS - 1)
                values(turn, 1, 0, TB)
                spread_rden(turn, 1)
                output(turn, PAIRS - 1, 1)

        @block.scalar
        def _(act):
            def prepare(p):
                act.activation(bias_now[:], bqk_sb[:, bass.ds(p, 1), :].rearrange("p a m -> p (a m)"), ACT.Copy)\
                   .then_inc(bias_in.sem, 1)
                w = w_raw[:, bass.ds(p, 1), :].rearrange("p a m -> p (a m)")
                act.activation(w_hi[:, 0:2 * P], w[:, 0:2 * P], ACT.Copy, scale=DH ** -0.5)\
                   .then_inc(w_split.sem, 1)
                act.activation(w_hi[:, 2 * P:], w[:, 2 * P:], ACT.Copy).then_inc(w_split.sem, 1)

            def exps(turn, i, hd):
                act.wait_ge(maxed.sem, maxed.at(turn, 2 * i + hd + 1))
                before = order[i - 1, hd, len(chunks(i - 1)) - 1] + 1 if i else 0
                act.wait_ge(turned.sem, turned.at(turn, before))
                act.activation(prob[:, hd, 0:(i + 1) * P], score[:, hd, 0:(i + 1) * P], ACT.Exp,
                               bias=negmax[:, hd, i:i + 1], accum_out=den[:, hd, i:i + 1]).then_inc(exped.sem, 1)

            def copy_av(turn, g):
                act.wait_ge(summed.sem, summed.at(turn, g + 1))
                act.activation(av_raw[:], av[:], ACT.Copy).then_inc(av_out.sem, 1)

            def copy(out, in_):
                return act.activation(out, in_, ACT.Copy)

            def body(turn, p, last):
                act.wait_ge(bias_in.sem, bias_in.at(turn, 1))
                act.sem_inc(k.passed, 1)
                for n in range(8):
                    act.wait_ge(proj.sem, proj.at(turn, n + 1))
                    to = (q_s if n < 4 else k_hi)[:, n // 2 % 2, n % 2 * CH:n % 2 * CH + CH]
                    act.activation(to, fresh[:, n % 4, :], ACT.Identity,
                                   bias=bias_now[:, n // 2:n // 2 + 1]).then_inc(hi_out.sem, 1)
                exps(turn, 0, 0)
                exps(turn, 0, 1)
                for i in range(TB):
                    for hd in range(2):
                        keep_turned(act, 0, kept_act, turn, i, hd, copy)
                        if i + 1 < TB:
                            exps(turn, i + 1, hd)
                        if (i, hd) == (2, 0) and last:
                            copy_av(turn - 1, 1)
                        if (i, hd) == (6, 0):
                            copy_av(turn, 0)
                    if i == 4:
                        act.wait_ge(v_proj.sem, v_proj.at(turn, 2))
                        act.sem_inc(k.passed, 1)
                        act.wait_ge(lo_out.sem, lo_out.at(turn, 8))
                        act.sem_inc(k.passed, 1)
                        prepare(p + 1)

            act.wait_ge(loaded.sem, 112)
            act.wait_ge(scaled.sem, 1)
            act.sem_inc(k.passed, 1)
            prepare(0)
            with act.Fori(0, BATCH) as b:
                act.wait_ge(v_proj.sem, v_proj.at(b * PAIRS, 0))
                act.sem_inc(k.passed, 1)
                act.activation(xb_hi[:], k.x_hi[:, bass.ds(b * SEQ, SEQ)].bitcast(F32), ACT.Copy)\
                   .then_inc(xb_kept.sem, 1)
                act.activation(xb_lo[:], k.x_lo[:, bass.ds(b * SEQ, SEQ)].bitcast(F32), ACT.Copy)\
                   .then_inc(xb_kept.sem, 1)
                body(b * PAIRS, 0, False)
                with act.Fori(1, PAIRS) as p:
                    body(b * PAIRS + p, p, True)
                copy_av(b * PAIRS + (PAIRS - 1), 1)

        @block.vector
        def _(dve):
            def prepare(turn, p):
                w = w_raw[:, bass.ds(p, 1), :].rearrange("p a m -> p (a m)")
                dve.wait_ge(w_split.sem, w_split.at(turn, 2))
                dve.scalar_tensor_tensor(out=w_lo[:, 0:2 * P], in0=w[:, 0:2 * P], scalar=DH ** -0.5,
                                         in1=w_hi[:, 0:2 * P].bitcast(F32), op0=ALU.mult, op1=ALU.subtract)\
                   .then_inc(w_rest.sem, 1)
                dve.tensor_tensor(w_lo[:, 2 * P:], w[:, 2 * P:], w_hi[:, 2 * P:].bitcast(F32), ALU.subtract)\
                   .then_inc(w_rest.sem, 1)

            def keep_v(turn, p, u):
                dve.wait_ge(v_proj.sem, v_proj.at(turn, u + 1))
                dve.tensor_tensor(v_sb[:, u * TC:(u + 1) * TC, :], rb[:].rearrange("p (t m) -> p t m", m=P),
                                  bv_b[:, bass.ds(p, 1), :].broadcast_to([P, TC, P]), ALU.add)\
                   .then_inc(v_out.sem, 1)

            def maxes(turn, i, hd):
                dve.wait_ge(scored.sem, scored.at(turn, 2 * i + hd + 1))
                dve.tensor_reduce(negmax[:, hd, i:i + 1], score[:, hd, 0:(i + 1) * P], AX.X, ALU.max,
                                  negate=True).then_inc(maxed.sem, 1)

            def rdens(turn, p, g):
                dve.wait_ge(exped.sem, exped.at(turn, 8 * g + 8))
                t = slice(g * TC, g * TC + TC)
                dve.tensor_tensor(den[:, :, t], den[:, :, t],
                                  ghost_b[:, bass.ds(p, 1), :].rearrange("p a h -> p h a")
                                  .broadcast_to([P, 2, TC]), ALU.add).then_inc(r_links.sem, 1)
                dve.wait_ge(r_links.sem, r_links.at(turn, 2 * g + 1))
                dve.reciprocal(rden[:, :, t], den[:, :, t]).then_inc(r_links.sem, 1)

            def normalised(turn, g):
                dve.wait_ge(spread.sem, spread.at(turn, g + 1))
                dve.wait_ge(av_out.sem, av_out.at(turn, g + 1))
                dve.wait_ge(outed.sem, outed.at(turn, g))
                dve.tensor_tensor(av_sb[:], rb[:], av_raw[:], ALU.mult).then_inc(av_done.sem, 1)

            def add_out(turn, b, g):
                dve.wait_ge(outed.sem, outed.at(turn, g + 1))
                out = k.resid[:, bass.ds(b * TB + g * TC, TC), :]
                dve.tensor_tensor(flat(out), flat(out), av[:], ALU.add).then_inc(added.sem, 1)

            def copy(out, in_):
                return dve.tensor_copy(out, in_)

            def body(turn, b, p, last):
                dve.wait_ge(bias_in.sem, bias_in.at(turn, 1))
                for n in range(8):
                    dve.wait_ge(hi_out.sem, hi_out.at(turn, n + 1))
                    hd, cols = n // 2 % 2, slice(n % 2 * CH, n % 2 * CH + CH)
                    bias = bias_now[:, n // 2:n // 2 + 1]
                    if n < 4:
                        low = slice(DH, P)
                        dve.scalar_tensor_tensor(out=q_s[low, hd, cols], in0=fresh[low, n % 4, :],
                                                 scalar=bias[low], in1=q_s[low, hd, cols].bitcast(F32),
                                                 op0=ALU.add, op1=ALU.subtract).then_inc(lo_out.sem, 1)
                    else:
                        dve.scalar_tensor_tensor(out=k_lo[:, hd, cols], in0=fresh[:, n % 4, :],
                                                 scalar=bias, in1=k_hi[:, hd, cols].bitcast(F32),
                                                 op0=ALU.add, op1=ALU.subtract).then_inc(lo_out.sem, 1)
                maxes(turn, 0, 0)
                maxes(turn, 0, 1)
                for i in range(TB):
                    for hd in range(2):
                        keep_turned(dve, 1, kept_dve, turn, i, hd, copy)
                        if i + 1 < TB:
                            maxes(turn, i + 1, hd)
                        if (i, hd) == (2, 0) and last:
                            normalised(turn - 1, 1)
                        if (i, hd) == (3, 1):
                            keep_v(turn, p, 0)
                            if last:
                                add_out(turn - 1, b, 1)
                            rdens(turn, p, 0)
                        if (i, hd) == (4, 1):
                            keep_v(turn, p, 1)
                        if (i, hd) == (6, 1):
                            normalised(turn, 0)
                            prepare(turn + 1, p + 1)
                        if (i, hd) == (7, 1):
                            add_out(turn, b, 0)
                rdens(turn, p, 1)

            dve.wait_ge(loaded.sem, 112)
            dve.tensor_scalar(bqk_sb[:, :, 0:2], bqk_sb[:, :, 0:2], DH ** -0.5, None, ALU.mult)\
               .then_inc(scaled.sem, 1)
            prepare(0, 0)
            with dve.Fori(0, BATCH) as b:
                body(b * PAIRS, b, 0, False)
                with dve.Fori(1, PAIRS) as p:
                    body(b * PAIRS + p, b, p, True)
                turn = b * PAIRS + (PAIRS - 1)
                normalised(turn, 1)
                add_out(turn, b, 1)


def second_norm_and_routing(nc, k, router_w, router_b, gates_dram):
    with ExitStack() as ctx:
        xn = sbuf(ctx, nc, "xn2", [P, TC, D])
        rw = sbuf(ctx, nc, "router_w_sb", [P, EXPERTS])
        rbias = sbuf(ctx, nc, "router_b_sb", [EXPERTS, 1])
        logT = sbuf(ctx, nc, "logits_t", [EXPERTS, CH])
        logits = sbuf(ctx, nc, "logits", [P, TILES, EXPERTS])
        best = sbuf(ctx, nc, "best", [P, TILES, 8])
        which = sbuf(ctx, nc, "which", [P, TILES, 8], U32)
        whichf = sbuf(ctx, nc, "which_f", [P, TILES, 2])
        number = sbuf(ctx, nc, "expert_number", [P, EXPERTS])
        gap = sbuf(ctx, nc, "gap", [P, TILES])
        second = sbuf(ctx, nc, "second", [P, TILES])
        gate = sbuf(ctx, nc, "gate", [P, 2, TILES])
        hit = [sbuf(ctx, nc, f"hit{i}", [P, TILES, EXPERTS]) for i in range(2)]
        gatesT = sbuf(ctx, nc, "gates_t", [EXPERTS, BATCH * SEQ])
        bank = [psum(ctx, nc, f"route_bank{i}", [P, CH]) for i in range(8)]

        loaded = Count(ctx, nc, "route_loaded")
        normed = Count(ctx, nc, "x2_normed", TC)
        turned = Count(ctx, nc, "x2_turned", 1, credit=1)
        state_out = Count(ctx, nc, "state_kept", 1)
        hi_out = Count(ctx, nc, "x2_hi_kept", 1, credit=1)
        lo_out = Count(ctx, nc, "x2_lo_kept", 1, credit=1)
        logit = Count(ctx, nc, "logits_ready", 1)
        log_out = Count(ctx, nc, "logits_biased", 1)
        log_turned = Count(ctx, nc, "logits_turned", 1)
        log_kept = Count(ctx, nc, "logits_kept", 1, credit=1)
        with nc.Block() as block:
            @block.sync
            def _(sp):
                sp.dma_start(rw[:], router_w).then_inc(loaded.sem, 16)
                sp.dma_start(rbias[:], router_b.rearrange("(e a) -> e a", a=1)).then_inc(loaded.sem, 16)

            @block.gpsimd
            def _(pool):
                for count in (turned, hi_out, lo_out, log_kept):
                    pool.sem_inc(count.sem, count.credit)

            @block.tensor
            def _(pe):
                pe.wait_ge(loaded.sem, 32)
                with pe.Fori(0, CHUNKS) as c:
                    pe.wait_ge(normed.sem, normed.at(c, TC))
                    pe.wait_ge(lo_out.sem, lo_out.at(c, 0))
                    for t in range(TC):
                        ins = pe.transpose(bank[0][:, t * P:(t + 1) * P], xn[:, t, :], k.ident[:])
                    ins.then_inc(turned.sem, 1)
                    pe.wait_ge(state_out.sem, state_out.at(c, 1))
                    pe.matmul(bank[1][0:EXPERTS, :], rw[:], k.state[:, bass.ds(c * CH, CH)], start=True, stop=True)\
                      .then_inc(logit.sem, 1)
                    pe.wait_ge(log_out.sem, log_out.at(c, 1))
                    pe.wait_ge(log_kept.sem, log_kept.at(c, 0))
                    pe.sem_inc(k.passed, 1)
                    for t in range(TC):
                        ins = pe.transpose(bank[2][:, t * EXPERTS:(t + 1) * EXPERTS], logT[:, t * P:(t + 1) * P],
                                           k.ident[0:EXPERTS, 0:EXPERTS])
                    ins.then_inc(log_turned.sem, 1)

            @block.scalar
            def _(act):
                act.wait_ge(loaded.sem, 32)
                with act.Fori(0, CHUNKS) as c:
                    act.wait_ge(turned.sem, turned.at(c, 1))
                    act.sem_inc(k.passed, 1)
                    cols = bass.ds(c * CH, CH)
                    act.activation(k.state[:, cols], bank[0][:], ACT.Copy).then_inc(state_out.sem, 1)
                    act.activation(k.x_hi[:, cols], bank[0][:], ACT.Copy).then_inc(hi_out.sem, 1)
                    act.wait_ge(logit.sem, logit.at(c, 1))
                    act.activation(logT[:], bank[1][0:EXPERTS, :], ACT.Identity, bias=rbias[:])\
                       .then_inc(log_out.sem, 1)

            @block.vector
            def _(dve):
                with dve.Fori(0, CHUNKS) as c:
                    dve.wait_ge(turned.sem, turned.at(c, 0))
                    normalise_chunk(dve, k, c, xn, normed)
                    dve.wait_ge(hi_out.sem, hi_out.at(c, 1))
                    dve.tensor_tensor(k.x_lo[:, bass.ds(c * CH, CH)], bank[0][:],
                                      k.x_hi[:, bass.ds(c * CH, CH)].bitcast(F32), ALU.subtract)\
                       .then_inc(lo_out.sem, 1)
                    dve.wait_ge(log_turned.sem, log_turned.at(c, 1))
                    dve.tensor_copy(flat(logits[:, bass.ds(c * TC, TC), :]), bank[2][:, 0:TC * EXPERTS])\
                       .then_inc(log_kept.sem, 1)

        numbered = Count(ctx, nc, "experts_numbered")
        found = Count(ctx, nc, "best_found")
        links = Count(ctx, nc, "gate_links")
        exped = Count(ctx, nc, "second_exped")
        gturned = Count(ctx, nc, "gates_turned")
        gkept = Count(ctx, nc, "gates_kept")
        stored = Count(ctx, nc, "gates_stored")
        with nc.Block() as block:
            @block.gpsimd
            def _(pool):
                for e in range(EXPERTS):
                    ins = pool.memset(number[:, e:e + 1], float(e))
                    ins.then_inc(numbered.sem, 1)

            @block.vector
            def _(dve):
                for t in range(TILES):
                    dve.max(best[:, t, :], logits[:, t, :]).then_inc(found.sem, 1)
                dve.wait_ge(found.sem, TILES)
                for t in range(TILES):
                    ins = dve.max_index(which[:, t, :], best[:, t, :], logits[:, t, :])
                ins.then_inc(found.sem, 1)
                chain = Chain(dve, links)
                link = chain.link
                link(dve.tensor_tensor(gap[:], best[:, :, 1], best[:, :, 0], ALU.subtract))
                dve.wait_ge(found.sem, TILES + 1)
                link(dve.tensor_copy(whichf[:], which[:, :, 0:2]))
                dve.wait_ge(exped.sem, 1)
                link(dve.tensor_scalar(gap[:], second[:], 1.0, None, ALU.add))
                link(dve.reciprocal(gate[:, 0, :], gap[:]))
                link(dve.tensor_tensor(gate[:, 1, :], second[:], gate[:, 0, :], ALU.mult))
                dve.wait_ge(numbered.sem, EXPERTS)
                shape = [P, TILES, EXPERTS]
                for i in range(2):
                    link(dve.tensor_tensor(hit[i][:], whichf[:, :, i:i + 1].broadcast_to(shape),
                                           number[:].unsqueeze(1).broadcast_to(shape), ALU.is_equal))
                    link(dve.tensor_tensor(hit[i][:], hit[i][:], gate[:, i, :].unsqueeze(2).broadcast_to(shape),
                                           ALU.mult))
                link(dve.tensor_tensor(hit[0][:], hit[0][:], hit[1][:], ALU.add))

            @block.scalar
            def _(act):
                act.wait_ge(links.sem, 1)
                act.activation(second[:], gap[:], ACT.Exp).then_inc(exped.sem, 1)
                for c in range(CHUNKS):
                    act.wait_ge(gturned.sem, c + 1)
                    act.activation(gatesT[:, c * CH:(c + 1) * CH], bank[c][0:EXPERTS, :], ACT.Copy)\
                       .then_inc(gkept.sem, 1)

            @block.tensor
            def _(pe):
                pe.wait_ge(links.sem, 10)
                for c in range(CHUNKS):
                    for t in range(TC):
                        ins = pe.transpose(bank[c][0:EXPERTS, t * P:(t + 1) * P], hit[0][:, c * TC + t, :],
                                           k.ident[:])
                    ins.then_inc(gturned.sem, 1)

            @block.sync
            def _(sp):
                sp.wait_ge(gkept.sem, CHUNKS)
                sp.dma_start(gates_dram, gatesT[:]).then_inc(stored.sem, 16)
                sp.wait_ge(stored.sem, 16)


(BQ, BK, BV, BO, S1, B1N, BF, B2F, S2, B2N) = (0, 1, 2, 3, 4, 5, 6, 10, 11, 12)
COLS = 13
K, Q = 0, 1


def linear_layers(nc, k, wqkv, wo, w1, w2, columns):
    with ExitStack() as ctx:
        wqkv_sb = [sbuf(ctx, nc, f"l_wqkv{u}", [P, 3, D]) for u in range(2)]
        wo_sb = [sbuf(ctx, nc, f"l_wo{u}", [P, D]) for u in range(2)]
        w1_sb = [sbuf(ctx, nc, f"l_w1{u}", [P, FF]) for u in range(2)]
        w2_sb = [sbuf(ctx, nc, f"l_w2{u}", [P, FC, D]) for u in range(2)]
        col = [sbuf(ctx, nc, f"l_col{u}", [P, COLS]) for u in range(2)]
        plus = [sbuf(ctx, nc, f"l_plus{u}", [P, 2]) for u in range(2)]
        eps_attn = sbuf(ctx, nc, "l_eps_attn", [P, 1])
        power = sbuf(ctx, nc, "l_power", [P, TC])
        ek = sbuf(ctx, nc, "l_ek", [P, 2, CH])
        kf = sbuf(ctx, nc, "l_kf", [P, 2, CH])
        junk = sbuf(ctx, nc, "l_junk", [P, 2, CH])
        eq = sbuf(ctx, nc, "l_eq", [P, 2, CH])
        q = sbuf(ctx, nc, "l_q", [P, CHUNKS, CH])
        yk = sbuf(ctx, nc, "l_yk", [P, 2, CH])
        sums = sbuf(ctx, nc, "l_sums", [P, 2, CHUNKS])
        tot = sbuf(ctx, nc, "l_tot", [P, 2, BATCH])
        ratio = sbuf(ctx, nc, "l_ratio", [P, BATCH])
        inv = sbuf(ctx, nc, "l_inv", [P, BATCH])
        less = sbuf(ctx, nc, "l_less", [P, BATCH])
        att = sbuf(ctx, nc, "l_att", [P, 2, CH])
        ff_out = sbuf(ctx, nc, "l_ff_out", [P, CH])
        x1 = sbuf(ctx, nc, "l_x1", [P, 2, CH])
        h = sbuf(ctx, nc, "l_h", [P, FC, CH])
        y = [sbuf(ctx, nc, f"l_y{s}", [P, 2, CH]) for s in range(2)]
        xhat = [sbuf(ctx, nc, f"l_xhat{s}", [P, 2, CH]) for s in range(2)]
        stats = [sbuf(ctx, nc, f"l_stats{s}", [P, 2, TC, 6]) for s in range(2)]
        mv = [sbuf(ctx, nc, f"l_mv{s}", [P, 2, TC, 2]) for s in range(2)]
        var = [sbuf(ctx, nc, f"l_var{s}", [P, 2, TC]) for s in range(2)]
        rstd = [sbuf(ctx, nc, f"l_rstd{s}", [P, 2, TC]) for s in range(2)]
        bank = [psum(ctx, nc, f"l_bank{i}", [P, CH]) for i in range(8)]

        N = 2 * CHUNKS
        TURNS = LAYERS // 2

        def count(name, per=N, credit=0):
            return Count(ctx, nc, f"l_{name}", per, credit)

        consts = count("consts", 0)
        w_in = [count(f"weights_in{u}", 16 * 5) for u in range(2)]
        plus_in = count("plus", 2)
        k_m, v_m, q_m = count("k_ready"), count("v_ready"), count("q_ready")
        clipped = {K: count("k_clipped"), Q: count("q_clipped")}
        exped = {K: count("k_exped"), Q: count("q_exped")}
        rounded = count("q_rounded")
        k_d, kv_d, q_d = count("k_summed"), count("kv_summed"), count("q_kept")
        tiny = count("ratio_links", 2 * BATCH * 5)
        ln_a, y_a, v_d = count("log_done"), count("inverse_done"), count("v_done")
        wo_m, att_a = count("wo_ready"), count("attn_gelu")
        add = [count(f"added{s}") for s in range(2)]
        t_a = [count(f"turned{s}") for s in range(2)]
        st = [count(f"stats{s}", N * TC) for s in range(2)]
        ag = [count(f"aggregated{s}") for s in range(2)]
        ve = [count(f"var_eps{s}") for s in range(2)]
        rs = [count(f"rstd{s}") for s in range(2)]
        nm = [count(f"normed{s}", credit=1) for s in range(2)]
        t_b = [count(f"turned_back{s}", credit=1) for s in range(2)]
        out = [count(f"x_out{s}") for s in range(2)]
        f1, hg = count("ff1_ready", N * FC), count("h_gelu", N * FC)
        f2, g2 = count("ff2_ready"), count("ff_gelu")

        block = ctx.enter_context(nc.Block())
        KB, QB_, WOV, TA, TA2, SHORT, F1 = 0, 1, 2, 3, 4, 5, 6

        D_WO, D_TA, D_TB, D_FF, D_TA2, D_TB2 = 3, 4, 5, 6, 7, 8

        class Slot:

            def __init__(self, eng, turn, n, lo, hi):
                self.eng, self.turn, self.n, self.lo, self.hi = eng, turn, n, lo, hi

            def runs(self, m):
                return self.lo <= m < self.hi

            def wait(self, count, m, of=1, k=1):
                if self.runs(m):
                    self.eng.wait_ge(count.sem, count.at(self.turn, m * of + k))

            def wait_weights(self, m):
                if m % CHUNKS == 0:
                    self.eng.wait_ge(w_in[m // CHUNKS % 2].sem, w_in[m // CHUNKS % 2].at(self.turn + m // N, 80))
                    self.eng.sem_inc(k.passed, 1)

        def pipeline(eng, slot):
            for n in range(D_TB2):
                slot(Slot(eng, 0, n, 0, N))
            with eng.Fori(0, TURNS - 1) as j:
                for n in range(D_TB2, D_TB2 + N):
                    slot(Slot(eng, j, n, 0, 2 * N))
            for n in range(D_TB2, D_TB2 + N):
                slot(Slot(eng, TURNS - 1, n, 0, N))

        def u_(m):
            return m // CHUNKS % 2

        @block.sync
        def _(sp):
            def load_layer(i, u, turn=None):
                def used(count, of=1):
                    if turn is not None:
                        sp.wait_ge(count.sem, count.at(turn, (u + 1) * CHUNKS * of))
                used(kv_d)
                used(q_d)
                if turn is not None:
                    sp.sem_inc(k.passed, 1)
                one = bass.ds(i, 1)
                sp.dma_start(wqkv_sb[u][:], wqkv[one].rearrange("a w k m -> k (a w) m")).then_inc(w_in[u].sem, 16)
                used(wo_m)
                sp.dma_start(wo_sb[u][:], wo[one].rearrange("a k m -> (a k) m")).then_inc(w_in[u].sem, 16)
                used(f1, FC)
                sp.dma_start(w1_sb[u][:], w1[one].rearrange("a k m -> (a k) m")).then_inc(w_in[u].sem, 16)
                used(f2)
                sp.dma_start(w2_sb[u][:], w2[one].rearrange("a (f k) m -> k (a f) m", k=P)).then_inc(w_in[u].sem, 16)
                used(out[1])
                sp.dma_start(col[u][:], columns[one].rearrange("a p c -> (a p) c")).then_inc(w_in[u].sem, 16)

            for u in range(2):
                load_layer(u, u)
            with sp.Fori(0, TURNS - 1) as j:
                for u in range(2):
                    load_layer(j * 2 + (u + 2), u, j)

        @block.gpsimd
        def _(pool):
            for c in (*nm, *t_b):
                pool.sem_inc(c.sem, c.credit)
            pool.memset(eps_attn[:], EPS_ATTN).then_inc(consts.sem, 1)
            pool.memset(power[:], -0.5).then_inc(consts.sem, 1)
            pool.wait_ge(consts.sem, 2)

            def slot(o):
                for s, m in ((1, o.n - D_TA2), (0, o.n - D_TA)):
                    if o.runs(m):
                        r = m % 2
                        o.wait(ag[s], m)
                        pool.sem_inc(k.passed, 1)
                        pool.tensor_scalar(var[s][:, r, :], mv[s][:, r, :, 1], EPS_LN, None, ALU.add)\
                            .then_inc(ve[s].sem, 1)
                        o.wait(ve[s], m)
                        o.wait(nm[s], m - 2)
                        pool.tensor_tensor(rstd[s][:, r, :], var[s][:, r, :], power[:], ALU.pow)\
                            .then_inc(rs[s].sem, 1)

            pipeline(pool, slot)

        @block.tensor
        def _(pe):
            def turn_tiles(to, src, signal):
                for t in range(TC):
                    ins = pe.transpose(to[:, t * P:(t + 1) * P], src[:, t * P:(t + 1) * P], k.ident[:])
                ins.then_inc(signal.sem, 1)

            def project(m, which, to, signal):
                c = m % CHUNKS
                pe.matmul(to[:], wqkv_sb[u_(m)][:, which, :], k.state[:, c * CH:(c + 1) * CH],
                          start=True, stop=True).then_inc(signal.sem, 1)

            def slot(o):
                def ff1(f):
                    m = o.n - D_FF
                    if o.runs(m):
                        o.wait(out[0], m)
                        o.wait(hg, m if f >= 2 else m - 1, FC, f - 1 if f >= 2 else f + 3)
                        pe.matmul(bank[F1 + f % 2][:], w1_sb[u_(m)][:, f * P:(f + 1) * P], x1[:, m % 2, :],
                                  start=True, stop=True).then_inc(f1.sem, 1)

                ff1(0)
                ff1(1)
                m = o.n - D_TB2
                if o.runs(m):
                    o.wait(nm[1], m)
                    o.wait(g2, m + 1)
                    o.wait(out[1], m - 1)
                    turn_tiles(bank[SHORT], xhat[1][:, m % 2, :], t_b[1])
                m = o.n - D_WO
                if o.runs(m):
                    o.wait(v_d, m)
                    o.wait(kv_d, o.n - 1)
                    pe.matmul(bank[WOV][:], wo_sb[u_(m)][:], q[:, m % CHUNKS, :], start=True, stop=True)\
                      .then_inc(wo_m.sem, 1)
                ff1(2)
                m = o.n
                if o.runs(m):
                    o.wait_weights(m)
                    o.wait(out[1], m - CHUNKS)
                    o.wait(k_d, m - 1)
                    project(m, 1, bank[KB], k_m)
                    o.wait(q_d, m - 1)
                    project(m, 0, bank[QB_], q_m)
                m = o.n - D_TA2
                if o.runs(m):
                    o.wait(add[1], m)
                    o.wait(nm[1], m - 1)
                    turn_tiles(bank[TA2], y[1][:, m % 2, :], t_a[1])
                ff1(3)
                m = o.n
                if o.runs(m):
                    o.wait(att_a, o.n - D_WO)
                    o.wait(kv_d, m - 1)
                    project(m, 2, bank[WOV], v_m)
                m = o.n - D_TB
                if o.runs(m):
                    o.wait(nm[0], m)
                    o.wait(out[1], o.n - D_TB2)
                    o.wait(g2, m - 2)
                    turn_tiles(bank[SHORT], xhat[0][:, m % 2, :], t_b[0])
                m = o.n - D_TA
                if o.runs(m):
                    o.wait(add[0], m)
                    o.wait(nm[0], m - 1)
                    turn_tiles(bank[TA], y[0][:, m % 2, :], t_a[0])
                m = o.n - D_FF
                if o.runs(m):
                    o.wait(out[0], o.n - D_TB)
                    o.wait(out[1], o.n - D_TB2)
                    for f in range(FC):
                        o.wait(hg, m, FC, f + 1)
                        ins = pe.matmul(bank[SHORT][:], w2_sb[u_(m)][:, f, :], h[:, f, :],
                                        start=(f == 0), stop=(f == FC - 1))
                    ins.then_inc(f2.sem, 1)

            pipeline(pe, slot)

        @block.scalar
        def _(act):
            def slot(o):
                def one(m, i):
                    return col[u_(m)][:, i:i + 1]

                def h_gelu(f):
                    m = o.n - D_FF
                    if o.runs(m):
                        if f == 0:
                            o.wait(f2, m - 1)
                        o.wait(f1, m, FC, f + 1)
                        act.activation(h[:, f, :], bank[F1 + f % 2][:], ACT.Gelu_apprx_tanh, bias=one(m, BF + f))\
                           .then_inc(hg.sem, 1)

                h_gelu(0)
                h_gelu(1)
                m = o.n - D_TB2
                if o.runs(m):
                    o.wait(t_b[1], m)
                    c = m % CHUNKS
                    act.activation(k.state[:, c * CH:(c + 1) * CH], bank[SHORT][:], ACT.Identity,
                                   bias=one(m, B2N), scale=one(m, S2)).then_inc(out[1].sem, 1)
                m = o.n - D_WO
                if o.runs(m):
                    o.wait_weights(m)
                    o.wait(wo_m, m)
                    o.wait(add[0], m - 2)
                    act.activation(att[:, m % 2, :], bank[WOV][:], ACT.Gelu_apprx_tanh, bias=one(m, BO))\
                       .then_inc(att_a.sem, 1)
                h_gelu(2)
                h_gelu(3)
                if o.n % 2 == 0 and o.runs(o.n - 2):
                    b = (o.n - 2) % CHUNKS // 2
                    pair = (o.n - 2, o.n - 1)
                    o.wait(tiny, (o.n - 2) // 2, 5, 5)
                    act.sem_inc(k.passed, 1)
                    for m in pair:
                        o.wait(q_d, m)
                        o.wait(v_d, m - 2)
                        act.activation(yk[:, m % 2, :], q[:, m % CHUNKS, :], ACT.Ln, bias=eps_attn[:],
                                       scale=tot[:, 0, b:b + 1]).then_inc(ln_a.sem, 1)
                    for m in pair:
                        o.wait(ln_a, m)
                        act.activation(yk[:, m % 2, :], yk[:, m % 2, :], ACT.Exp, scale=-1.0).then_inc(y_a.sem, 1)
                m = o.n
                if o.runs(m):
                    for which, buf in ((K, ek), (Q, eq)):
                        o.wait(clipped[which], m)
                        act.activation(buf[:, m % 2, :], buf[:, m % 2, :], ACT.Exp).then_inc(exped[which].sem, 1)
                m = o.n - D_FF
                if o.runs(m):
                    o.wait(f2, m)
                    o.wait(add[1], m - 1)
                    act.activation(ff_out[:], bank[SHORT][:], ACT.Gelu_apprx_tanh, bias=one(m, B2F))\
                       .then_inc(g2.sem, 1)

            act.wait_ge(consts.sem, 2)
            act.sem_inc(k.passed, 1)
            pipeline(act, slot)

        @block.vector
        def _(dve):
            def statistics(o, s, b_, m):
                r = m % 2
                o.wait(t_a[s], m)
                for t in range(TC):
                    dve.bn_stats(stats[s][:, r, t, :], b_[:, t * P:(t + 1) * P]).then_inc(st[s].sem, 1)
                o.wait(st[s], m, TC, TC)
                dve.sem_inc(k.passed, 1)
                for t in range(TC):
                    ins = dve.bn_aggr(mv[s][:, r, t, :], stats[s][:, r, t, :])
                ins.then_inc(ag[s].sem, 1)

            def normalise(o, s, b_, m):
                r = m % 2
                o.wait(rs[s], m)
                o.wait(t_b[s], m - 2)
                for t in range(TC):
                    cols = slice(t * P, t * P + P)
                    ins = dve.tensor_scalar(xhat[s][:, r, cols], b_[:, cols], mv[s][:, r, t, 0:1],
                                            rstd[s][:, r, t:t + 1], ALU.subtract, ALU.mult)
                ins.then_inc(nm[s].sem, 1)

            def slot(o):
                m = o.n - D_TB
                if o.runs(m):
                    normalise(o, 0, bank[TA], m)
                if o.n % 2 and o.runs(o.n - 3):
                    for m in (o.n - 3, o.n - 2):
                        b = m % CHUNKS // 2
                        o.wait(y_a, m)
                        dve.tensor_scalar(q[:, m % CHUNKS, :], yk[:, m % 2, :], less[:, b:b + 1], ratio[:, b:b + 1],
                                          ALU.mult, ALU.add).then_inc(v_d.sem, 1)
                m = o.n - 1
                if o.runs(m):
                    r, c, u = m % 2, m % CHUNKS, u_(m)
                    o.wait(exped[K], m)
                    o.wait(kv_d, m - 2)
                    dve.scalar_tensor_tensor(out=kf[:, r, :], in0=bank[KB][:], scalar=plus[u][:, 1:2],
                                             in1=ek[:, r, :], op0=ALU.add, op1=ALU.max,
                                             accum_out=sums[:, 0, c:c + 1]).then_inc(k_d.sem, 1)
                    o.wait(exped[Q], m)
                    dve.tensor_scalar(eq[:, r, :], eq[:, r, :], 1.0, 1.0, ALU.subtract, ALU.add)\
                       .then_inc(rounded.sem, 1)
                    o.wait(v_m, m)
                    o.wait(k_d, m)
                    dve.scalar_tensor_tensor(out=junk[:, r, :], in0=bank[WOV][:], scalar=col[u][:, BV:BV + 1],
                                             in1=kf[:, r, :], op0=ALU.add, op1=ALU.mult,
                                             accum_out=sums[:, 1, c:c + 1]).then_inc(kv_d.sem, 1)
                    o.wait(rounded, m)
                    dve.scalar_tensor_tensor(out=q[:, c, :], in0=bank[QB_][:], scalar=plus[u][:, 0:1],
                                             in1=eq[:, r, :], op0=ALU.add, op1=ALU.max).then_inc(q_d.sem, 1)
                    if m % 2:
                        b = c // 2
                        one = slice(b, b + 1)
                        o.wait(kv_d, m)
                        chain = Chain(dve, tiny, o.turn)
                        chain.n = m // 2 * 5
                        chain.link(dve.tensor_tensor(tot[:, :, b], sums[:, :, c - 1], sums[:, :, c], ALU.add))
                        chain.link(dve.tensor_scalar(inv[:, one], tot[:, 0, one], 1e-30, None, ALU.max))
                        chain.link(dve.reciprocal(inv[:, one], inv[:, one]))
                        chain.link(dve.tensor_tensor(ratio[:, one], tot[:, 1, one], inv[:, one], ALU.mult))
                        chain.link(dve.tensor_scalar(less[:, one], ratio[:, one], -EPS_ATTN, None, ALU.mult))
                m = o.n - D_TA2
                if o.runs(m):
                    o.wait(g2, m)
                    o.wait(t_a[1], m - 2)
                    dve.tensor_tensor(y[1][:, m % 2, :], ff_out[:], x1[:, m % 2, :], ALU.add).then_inc(add[1].sem, 1)
                m = o.n - D_WO
                if o.runs(m):
                    o.wait(att_a, m)
                    o.wait(t_a[0], m - 2)
                    c = m % CHUNKS
                    dve.tensor_tensor(y[0][:, m % 2, :], att[:, m % 2, :], k.state[:, c * CH:(c + 1) * CH],
                                      ALU.add).then_inc(add[0].sem, 1)
                m = o.n
                if o.runs(m):
                    r, u = m % 2, u_(m)
                    if m % CHUNKS == 0:
                        o.wait_weights(m)
                        dve.tensor_scalar(plus[u][:], col[u][:, 0:2], 1.0, None, ALU.add).then_inc(plus_in.sem, 1)
                        dve.wait_ge(plus_in.sem, plus_in.at(o.turn, m // CHUNKS + 1))
                    for which, buf, src, ready, done, bias in ((K, ek, KB, k_m, k_d, BK), (Q, eq, QB_, q_m, q_d, BQ)):
                        o.wait(ready, m)
                        o.wait(done, m - 2)
                        dve.tensor_scalar(buf[:, r, :], bank[src][:], col[u][:, bias:bias + 1], 0.0,
                                          ALU.add, ALU.min).then_inc(clipped[which].sem, 1)
                m = o.n - D_TA2
                if o.runs(m):
                    statistics(o, 1, bank[TA2], m)
                m = o.n - D_TB
                if o.runs(m):
                    o.wait(t_b[0], m)
                    o.wait(add[1], m - 2)
                    dve.tensor_scalar(x1[:, m % 2, :], bank[SHORT][:], col[u_(m)][:, S1:S1 + 1],
                                      col[u_(m)][:, B1N:B1N + 1], ALU.mult, ALU.add).then_inc(out[0].sem, 1)
                m = o.n - D_TA
                if o.runs(m):
                    statistics(o, 0, bank[TA], m)
                m = o.n - D_TA2
                if o.runs(m):
                    normalise(o, 1, bank[TA2], m)

            pipeline(dve, slot)


def experts(nc, k, w1, w2, columns, gates_dram):
    CB1, CB2 = 0, FC
    with ExitStack() as ctx:
        w1_raw = [sbuf(ctx, nc, f"e_w1_raw{u}", [P, FF]) for u in range(2)]
        w2_raw = [sbuf(ctx, nc, f"e_w2_raw{u}", [P, FC, D]) for u in range(2)]
        w1_hi = [sbuf(ctx, nc, f"e_w1_hi{u}", [P, FF], F32R) for u in range(2)]
        w1_lo = [sbuf(ctx, nc, f"e_w1_lo{u}", [P, FF], F32R) for u in range(2)]
        w2_hi = [sbuf(ctx, nc, f"e_w2_hi{u}", [P, FC, D], F32R) for u in range(2)]
        w2_lo = [sbuf(ctx, nc, f"e_w2_lo{u}", [P, FC, D], F32R) for u in range(2)]
        col = [sbuf(ctx, nc, f"e_col{u}", [P, FC + 1]) for u in range(2)]
        gate_b = sbuf(ctx, nc, "e_gate_b", [P, 4, CH])
        h = sbuf(ctx, nc, "e_h", [P, 2, FC, CH])
        h_hi = sbuf(ctx, nc, "e_h_hi", [P, 2, FC, CH], F32R)
        h_lo = sbuf(ctx, nc, "e_h_lo", [P, 2, FC, CH], F32R)
        gated = sbuf(ctx, nc, "e_gated", [P, 2, CH])
        bank = [psum(ctx, nc, f"e_bank{i}", [P, CH]) for i in range(8)]
        N = 2 * CHUNKS

        def count(name, per=N, credit=0):
            return Count(ctx, nc, f"e_{name}", per, credit)

        w_in = [count(f"weights_in{u}", 16 * 3) for u in range(2)]
        g_in = [count(f"gates_in{i}", 16 * N // 4) for i in range(4)]
        w_hi = count("w_hi", 4)
        w_lo = count("w_lo", 4, credit=4)
        f1 = count("ff1_ready", N * FC)
        hg = count("h_gelu", N * FC, credit=4)
        hh = count("h_hi", N * FC)
        hl = count("h_lo", N * FC, credit=8)
        f2 = count("ff2_ready", N, credit=9)
        yg = count("gated", N, credit=9)
        ya = count("gate_added", N, credit=2)
        block = ctx.enter_context(nc.Block())

        @block.sync
        def _(sp):
            with sp.Fori(0, EXPERTS // 2) as j:
                for u in range(2):
                    sp.wait_ge(w_lo.sem, w_lo.at(j, 2 * u - 2))
                    sp.wait_ge(yg.sem, yg.at(j, (u - 1) * CHUNKS))
                    sp.sem_inc(k.passed, 1)
                    one = bass.ds(j * 2 + u, 1)
                    sp.dma_start(w1_raw[u][:], w1[one].rearrange("a k m -> (a k) m")).then_inc(w_in[u].sem, 16)
                    sp.dma_start(w2_raw[u][:], w2[one].rearrange("a (f k) m -> k (a f) m", k=P)).then_inc(w_in[u].sem, 16)
                    sp.dma_start(col[u][:], columns[one].rearrange("a p c -> (a p) c")).then_inc(w_in[u].sem, 16)
                    for c in range(CHUNKS):
                        n = u * CHUNKS + c
                        sp.wait_ge(yg.sem, yg.at(j, n - 3))
                        sp.sem_inc(k.passed, 1)
                        sp.dma_start(gate_b[:, c % 4, :], gates_dram[one, c * CH:(c + 1) * CH].broadcast_to([P, CH]))\
                          .then_inc(g_in[c % 4].sem, 16)

        @block.gpsimd
        def _(pool):
            for c in (w_lo, hg, hl, f2, yg, ya):
                pool.sem_inc(c.sem, c.credit)

        @block.tensor
        def _(pe):
            with pe.Fori(0, EXPERTS // 2) as j:
                for u in range(2):
                    def up(c):
                        n = u * CHUNKS + c
                        cols = slice(c * CH, c * CH + CH)
                        for f in range(FC):
                            pe.wait_ge(hg.sem, hg.at(j, n * FC + f - 3))
                            w = slice(f * P, f * P + P)
                            pe.matmul(bank[f][:], w1_hi[u][:, w], k.x_hi[:, cols], start=True, stop=False)
                            pe.matmul(bank[f][:], w1_hi[u][:, w], k.x_lo[:, cols], start=False, stop=False)
                            pe.matmul(bank[f][:], w1_lo[u][:, w], k.x_hi[:, cols], start=False, stop=True)\
                              .then_inc(f1.sem, 1)

                    def down(c):
                        n, r = u * CHUNKS + c, c % 2
                        pe.wait_ge(yg.sem, yg.at(j, n - 1))
                        for f in range(FC):
                            pe.wait_ge(hl.sem, hl.at(j, n * FC + f + 1))
                            pe.matmul(bank[4 + r][:], w2_hi[u][:, f, :], h_hi[:, r, f, :], start=(f == 0), stop=False)
                            pe.matmul(bank[4 + r][:], w2_hi[u][:, f, :], h_lo[:, r, f, :], start=False, stop=False)
                            ins = pe.matmul(bank[4 + r][:], w2_lo[u][:, f, :], h_hi[:, r, f, :], start=False,
                                            stop=(f == FC - 1))
                        ins.then_inc(f2.sem, 1)

                    pe.wait_ge(w_hi.sem, w_hi.at(j, 2 * u + 2))
                    pe.wait_ge(w_lo.sem, w_lo.at(j, 2 * u + 2))
                    for c in range(CHUNKS + 1):
                        if c < CHUNKS:
                            up(c)
                        if c:
                            down(c - 1)

        @block.scalar
        def _(act):
            with act.Fori(0, EXPERTS // 2) as j:
                for u in range(2):
                    act.wait_ge(w_in[u].sem, w_in[u].at(j, 48))
                    act.wait_ge(f2.sem, f2.at(j, (u - 1) * CHUNKS))
                    act.activation(w1_hi[u][:], w1_raw[u][:], ACT.Copy).then_inc(w_hi.sem, 1)
                    act.activation(w2_hi[u][:], w2_raw[u][:], ACT.Copy).then_inc(w_hi.sem, 1)
                    for c in range(CHUNKS):
                        n, r = u * CHUNKS + c, c % 2
                        for f in range(FC):
                            act.wait_ge(f1.sem, f1.at(j, n * FC + f + 1))
                            act.wait_ge(hl.sem, hl.at(j, n * FC + f - 7))
                            act.activation(h[:, r, f, :], bank[f][:], ACT.Gelu, bias=col[u][:, CB1 + f:CB1 + f + 1])\
                               .then_inc(hg.sem, 1)

        @block.vector
        def _(dve):
            with dve.Fori(0, EXPERTS // 2) as j:
                for u in range(2):
                    def combine(c):
                        n, r = u * CHUNKS + c, c % 2
                        dve.wait_ge(f2.sem, f2.at(j, n + 1))
                        dve.wait_ge(g_in[c % 4].sem, g_in[c % 4].at(j, 16 * (u * 2 + c // 4 + 1)))
                        dve.wait_ge(ya.sem, ya.at(j, n - 1))
                        dve.scalar_tensor_tensor(out=gated[:, r, :], in0=bank[4 + r][:],
                                                 scalar=col[u][:, CB2:CB2 + 1], in1=gate_b[:, c % 4, :],
                                                 op0=ALU.add, op1=ALU.mult).then_inc(yg.sem, 1)
                        dve.wait_ge(yg.sem, yg.at(j, n + 1))
                        s = k.state[:, c * CH:(c + 1) * CH]
                        dve.tensor_tensor(s, s, gated[:, r, :], ALU.add).then_inc(ya.sem, 1)

                    dve.wait_ge(w_hi.sem, w_hi.at(j, 2 * u + 2))
                    dve.wait_ge(f2.sem, f2.at(j, (u - 1) * CHUNKS))
                    for lo, raw, hi in ((w1_lo, w1_raw, w1_hi), (w2_lo, w2_raw, w2_hi)):
                        dve.tensor_tensor(lo[u][:], raw[u][:], hi[u][:].bitcast(F32), ALU.subtract)\
                           .then_inc(w_lo.sem, 1)
                    for c in range(CHUNKS):
                        n, r = u * CHUNKS + c, c % 2
                        dve.wait_ge(f2.sem, f2.at(j, n - 1))
                        for f in range(FC):
                            dve.wait_ge(hg.sem, hg.at(j, n * FC + f + 1))
                            dve.tensor_copy(h_hi[:, r, f, :], h[:, r, f, :]).then_inc(hh.sem, 1)
                            dve.wait_ge(hh.sem, hh.at(j, n * FC + f + 1))
                            dve.tensor_tensor(h_lo[:, r, f, :], h[:, r, f, :], h_hi[:, r, f, :].bitcast(F32),
                                              ALU.subtract).then_inc(hl.sem, 1)
                        if c:
                            combine(c - 1)
                    combine(CHUNKS - 1)


def write_out(nc, k, out):
    with ExitStack() as ctx:
        bank = [psum(ctx, nc, f"o_bank{i}", [P, CH]) for i in range(CHUNKS)]
        turned = Count(ctx, nc, "o_turned")
        added = Count(ctx, nc, "o_added")
        stored = Count(ctx, nc, "o_stored")
        block = ctx.enter_context(nc.Block())

        @block.tensor
        def _(pe):
            for c in range(CHUNKS):
                for t in range(TC):
                    at = c * CH + t * P
                    ins = pe.transpose(bank[c][:, t * P:(t + 1) * P], k.state[:, at:at + P], k.ident[:])
                ins.then_inc(turned.sem, 1)

        @block.vector
        def _(dve):
            for c in range(CHUNKS):
                dve.wait_ge(turned.sem, c + 1)
                r = flat(k.resid[:, c * TC:(c + 1) * TC, :])
                dve.tensor_tensor(r, r, bank[c][:], ALU.add).then_inc(added.sem, 1)

        @block.sync
        def _(sp):
            for c in range(CHUNKS):
                sp.wait_ge(added.sem, c + 1)
                sp.dma_start(out[c * CH:(c + 1) * CH, :].rearrange("(t p) d -> p t d", p=P),
                             k.resid[:, c * TC:(c + 1) * TC, :]).then_inc(stored.sem, 16)
            sp.wait_ge(stored.sem, 16 * CHUNKS)


class Kept:
    pass


def program(nc, x, wqkv, bqk, bv, wo, wo_bias, ghost, w_gate, w_up, w_down,
            l_wqkv, l_wo, l_w1, l_w2, l_columns, router_w, router_b, e_w1, e_w2, e_columns, out):
    with ExitStack() as ctx:
        k = Kept()
        k.passed = ctx.enter_context(nc.semaphore("waits_passed"))
        k.ident = sbuf(ctx, nc, "ident", [P, P])
        k.identb = sbuf(ctx, nc, "identb", [P, P], BF16)
        k.maskb = sbuf(ctx, nc, "maskb", [P, P], BF16)
        k.eps_outer = sbuf(ctx, nc, "eps_outer", [P, 1])
        k.eps_ln = sbuf(ctx, nc, "eps_ln", [P, 1])
        k.resid = sbuf(ctx, nc, "resid", [P, TILES, D])
        k.mv = sbuf(ctx, nc, "mean_var", [P, TILES, 2])
        k.rstd = sbuf(ctx, nc, "rstd", [P, TILES])
        k.x_hi = sbuf(ctx, nc, "x_hi", [P, BATCH * SEQ], F32R)
        k.x_lo = sbuf(ctx, nc, "x_lo", [P, BATCH * SEQ], F32R)
        gates_dram = nc.dram_tensor("gates_dram", [EXPERTS, BATCH * SEQ], F32, kind="Internal").ap()

        build_constants(nc, k)
        load(nc, k, x)
        outer_statistics(nc, k, "n1")
        quantized_feed_forward(nc, k, w_gate, w_up, w_down, wo_bias)
        attention(nc, k, wqkv, bqk, bv, wo, ghost)
        outer_statistics(nc, k, "n2")
        k.state = sbuf(ctx, nc, "state", [P, BATCH * SEQ])
        second_norm_and_routing(nc, k, router_w, router_b, gates_dram)
        linear_layers(nc, k, l_wqkv, l_wo, l_w1, l_w2, l_columns)
        experts(nc, k, e_w1, e_w2, e_columns, gates_dram)
        write_out(nc, k, out)


def load(nc, k, x):
    with ExitStack() as ctx:
        loaded = Count(ctx, nc, "x_loaded")
        block = ctx.enter_context(nc.Block())

        @block.sync
        def _(sp):
            for b in range(BATCH):
                sp.dma_start(k.resid[:, b * TB:(b + 1) * TB, :],
                             x[b * SEQ:(b + 1) * SEQ, :].rearrange("(t p) d -> p t d", p=P)).then_inc(loaded.sem, 16)
            sp.wait_ge(loaded.sem, 16 * BATCH)


def kernel(**inputs):
    import numpy as np
    import concourse.bacc as bacc
    from concourse.bass_utils import run_bass_kernel_spmd

    a = {n: np.asarray(v) for n, v in inputs.items()}
    wt = a["L0_attn_Wqkv_w"].T.reshape(D, 3, PAIRS, 2, DH)
    qk = np.repeat(wt[:, :2].transpose(2, 0, 1, 3, 4)[:, :, :, :, None, :], 2, axis=4).reshape(PAIRS, D, 4 * P)
    v = wt[:, 2].transpose(1, 0, 2, 3).reshape(PAIRS, D, P)
    bt = a["L0_attn_Wqkv_b"].reshape(3, PAIRS, 2, DH)
    bqk = np.repeat(bt[:2].transpose(1, 0, 2, 3)[:, :, :, None, :], 2, axis=3).reshape(PAIRS, 4, P)
    l = {n[8:]: v_ for n, v_ in a.items() if n.startswith("L1_attn_")}
    l_columns = np.stack([l["bq"], l["bk"], l["bv"], l["bo"], l["ln1_s"], l["ln1_b"],
                          *l["b1"].reshape(LAYERS, FC, P).transpose(1, 0, 2), l["b2"], l["ln2_s"], l["ln2_b"]],
                         axis=-1)
    e_columns = np.stack([*a["L1_ffn_b1"].reshape(EXPERTS, FC, P).transpose(1, 0, 2), a["L1_ffn_b2"]], axis=-1)
    arrays = {
        "x": a["L0_attn_inputs"].reshape(BATCH * SEQ, D), "wqkv": np.concatenate([qk, v], axis=2),
        "bqk": bqk.transpose(0, 2, 1), "bv": bt[2].reshape(-1), "wo": a["L0_attn_Wo_w"].T,
        "wo_bias": a["L0_attn_Wo_b"], "ghost": a["L0_attn_ghost"],
        "w_gate": a["L0_ffn_w_gate"], "w_up": a["L0_ffn_w_up"], "w_down": a["L0_ffn_w_down"],
        "l_wqkv": np.stack([l["Wq"], l["Wk"], l["Wv"]], axis=1), "l_wo": l["Wo"], "l_w1": l["W1"], "l_w2": l["W2"],
        "l_columns": l_columns, "router_w": a["L1_ffn_router_w"], "router_b": a["L1_ffn_router_b"],
        "e_w1": a["L1_ffn_w1"], "e_w2": a["L1_ffn_w2"], "e_columns": e_columns,
    }
    arrays = {n: np.ascontiguousarray(v_) for n, v_ in arrays.items()}
    nc = bacc.Bacc("TRN2", target_bir_lowering=False, num_devices=1)
    args = {n: nc.dram_tensor(f"in_{n}", v_.shape, mybir.dt.from_np(v_.dtype), kind="ExternalInput").ap()
            for n, v_ in arrays.items()}
    out = nc.dram_tensor("out", [BATCH * SEQ, D], F32, kind="ExternalOutput").ap()
    program(nc, out=out, **args)
    r = run_bass_kernel_spmd(nc, [{f"in_{n}": v_ for n, v_ in arrays.items()}], core_ids=[0])
    return r.results[0]["out"].reshape(BATCH, SEQ, D)
```
